# Optimizing a Trainium2 kernel written in Bass

```python
import numpy as np
import jax
import jax.numpy as jnp

def _softmax(x, axis=-1):
    return jax.nn.softmax(x, axis=axis)

def _gelu(x):
    return jax.nn.gelu(x, approximate=True)

def _silu(x):
    return jax.nn.silu(x)

def _sigmoid(x):
    return jax.nn.sigmoid(x)

def _layernorm(x, axis=-1, eps=1e-05):
    m = jnp.mean(x, axis=axis, keepdims=True)
    v = jnp.var(x, axis=axis, keepdims=True)
    return (x - m) / jnp.sqrt(v + eps)

def _scatter_add(tgt, idx, src, axis=0):
    return tgt.at[idx].add(src)

def _segment_sum(src, seg, n):
    return jax.ops.segment_sum(src, seg, n)
kernel_name = 'mk_sandwich_d1_jaxref_r4_667b44'

def setup_inputs(seed: int=0):
    np.random.seed(seed)
    _w = jnp.asarray

    def _L0_attn_setup():
        import jax, jax.numpy as jnp
        import numpy as np
        B, T, DM, H, DH = (4, 512, 256, 16, 64)
        DI = H * DH
        CLIP = 1.0
        LN_EPS = 1e-05
        key = jax.random.key(seed)
        ks = jax.random.split(key, 9)

        def xav(k, shape):
            lim = float(np.sqrt(6.0 / (shape[0] + shape[1])))
            return jax.random.uniform(k, shape, jnp.float32, -lim, lim)

        def kai(k, shape):
            lim = float(1.0 / np.sqrt(shape[1]))
            return jax.random.uniform(k, shape, jnp.float32, -lim, lim)
        return {'x': jax.random.normal(ks[0], (B, T, DM), jnp.float32), 'Wq': xav(ks[1], (DI, DM)), 'Wk': xav(ks[2], (DI, DM)), 'Wv': xav(ks[3], (DI, DM)), 'Wa': kai(ks[4], (DI, DM)), 'ba': jnp.full((DI,), 3.0, jnp.float32), 'Wb': kai(ks[5], (H, DM)), 'bb': jnp.zeros((H,), jnp.float32), 'Wg': kai(ks[6], (H, DM)), 'bg': jnp.zeros((H,), jnp.float32), 'WaR': kai(ks[7], (DI, DM)), 'baR': jnp.full((DI,), 3.0, jnp.float32), 'Wo': xav(ks[8], (DM, DI)), 'ln_w': jnp.ones((DM,), jnp.float32), 'ln_b': jnp.zeros((DM,), jnp.float32)}
    _L0_attn_in = _L0_attn_setup()

    def _L0_ffn_setup():
        import jax, jax.numpy as jnp
        import numpy as np
        H = 256
        I = 128
        E = 64
        G = 8
        TOPK_GROUP = 4
        K = 8
        I_SH = 256
        SCALE = 2.5

        def _route(x, router_w, e_bias):
            T = x.shape[0]
            scores = jax.nn.sigmoid(x.astype(jnp.float32) @ router_w.T.astype(jnp.float32))
            sfc = jax.lax.stop_gradient(scores) + e_bias[None, :]
            group_scores = jax.lax.top_k(sfc.reshape(T, G, E // G), 2)[0].sum(-1)
            _, gidx = jax.lax.top_k(group_scores, TOPK_GROUP)
            gmask = jax.nn.one_hot(gidx, G, dtype=sfc.dtype).sum(1)
            smask = jnp.repeat(gmask, E // G, axis=1)
            masked = jnp.where(smask > 0, sfc, 0.0)
            _, topk_idx = jax.lax.top_k(masked, K)
            w = jnp.take_along_axis(scores, topk_idx, axis=1)
            w = w / (w.sum(-1, keepdims=True) + 1e-20)
            return (topk_idx, w * SCALE)
        key = jax.random.key(seed)
        ks = jax.random.split(key, 9)
        s = 0.02
        return {'hidden_states': jax.random.normal(ks[0], (2, 256, H), jnp.float32), 'router_w': jax.random.normal(ks[1], (E, H), jnp.float32) * s, 'e_bias': jnp.zeros((E,), jnp.float32), 'Wg': jax.random.normal(ks[2], (E, H, I), jnp.float32) * s, 'Wu': jax.random.normal(ks[3], (E, H, I), jnp.float32) * s, 'Wd': jax.random.normal(ks[4], (E, I, H), jnp.float32) * s, 'SWg': jax.random.normal(ks[5], (H, I_SH), jnp.float32) * s, 'SWu': jax.random.normal(ks[6], (H, I_SH), jnp.float32) * s, 'SWd': jax.random.normal(ks[7], (I_SH, H), jnp.float32) * s}
    _L0_ffn_in = _L0_ffn_setup()
    _d = {'L0_attn_x': _L0_attn_in['x'], 'L0_attn_Wq': _L0_attn_in['Wq'], 'L0_attn_Wk': _L0_attn_in['Wk'], 'L0_attn_Wv': _L0_attn_in['Wv'], 'L0_attn_Wa': _L0_attn_in['Wa'], 'L0_attn_ba': _L0_attn_in['ba'], 'L0_attn_Wb': _L0_attn_in['Wb'], 'L0_attn_bb': _L0_attn_in['bb'], 'L0_attn_Wg': _L0_attn_in['Wg'], 'L0_attn_bg': _L0_attn_in['bg'], 'L0_attn_WaR': _L0_attn_in['WaR'], 'L0_attn_baR': _L0_attn_in['baR'], 'L0_attn_Wo': _L0_attn_in['Wo'], 'L0_attn_ln_w': _L0_attn_in['ln_w'], 'L0_attn_ln_b': _L0_attn_in['ln_b'], 'L0_ffn_router_w': _L0_ffn_in['router_w'], 'L0_ffn_e_bias': _L0_ffn_in['e_bias'], 'L0_ffn_Wg': _L0_ffn_in['Wg'], 'L0_ffn_Wu': _L0_ffn_in['Wu'], 'L0_ffn_Wd': _L0_ffn_in['Wd'], 'L0_ffn_SWg': _L0_ffn_in['SWg'], 'L0_ffn_SWu': _L0_ffn_in['SWu'], 'L0_ffn_SWd': _L0_ffn_in['SWd']}
    _x0 = _d['L0_attn_x']
    _d['L0_attn_x'] = jax.random.normal(jax.random.fold_in(jax.random.key(seed), 1), (2, 2048, 256), dtype=_x0.dtype)
    del _x0
    return _d

def reference(L0_attn_x, L0_attn_Wq, L0_attn_Wk, L0_attn_Wv, L0_attn_Wa, L0_attn_ba, L0_attn_Wb, L0_attn_bb, L0_attn_Wg, L0_attn_bg, L0_attn_WaR, L0_attn_baR, L0_attn_Wo, L0_attn_ln_w, L0_attn_ln_b, L0_ffn_router_w, L0_ffn_e_bias, L0_ffn_Wg, L0_ffn_Wu, L0_ffn_Wd, L0_ffn_SWg, L0_ffn_SWu, L0_ffn_SWd):

    def _L0_attn_ref(x, Wq, Wk, Wv, Wa, ba, Wb, bb, Wg, bg, WaR, baR, Wo, ln_w, ln_b):
        import jax, jax.numpy as jnp
        import numpy as np
        B, T, DM, H, DH = (4, 512, 256, 16, 64)
        DI = H * DH
        CLIP = 1.0
        LN_EPS = 1e-05
        Bs, Ts, _ = x.shape
        residual = x
        mu = jnp.mean(x, -1, keepdims=True)
        var = jnp.mean((x - mu) ** 2, -1, keepdims=True)
        xn = (x - mu) / jnp.sqrt(var + LN_EPS) * ln_w + ln_b
        q = (xn @ Wq.T).reshape(Bs, Ts, H, DH)
        k = (xn @ Wk.T).reshape(Bs, Ts, H, DH)
        v = (xn @ Wv.T).reshape(Bs, Ts, H, DH)
        alpha = jax.nn.sigmoid(xn @ Wa.T + ba).reshape(Bs, Ts, H, DH)
        aR = jax.nn.sigmoid(xn @ WaR.T + baR).reshape(Bs, Ts, H, DH)
        beta = jax.nn.sigmoid(xn @ Wb.T + bb)
        gamma = jax.nn.sigmoid(xn @ Wg.T + bg)
        tm = lambda a: jnp.moveaxis(a, 1, 0)
        xs = (tm(q), tm(k), tm(v), tm(alpha), tm(aR), tm(beta), tm(gamma))
        S0 = jnp.zeros((Bs, H, DH, DH), x.dtype)

        def step(carry, inp):
            S, R = carry
            q_t, k_t, v_t, a_t, aR_t, b_t, g_t = inp
            kn = k_t / jnp.maximum(jnp.linalg.norm(k_t, axis=-1, keepdims=True), 1e-12)
            pred = jnp.einsum('bhji,bhj->bhi', S, kn)
            r = jnp.clip(v_t - pred, -CLIP, CLIP)
            S = a_t[..., None] * S
            kp = jnp.einsum('bhd,bhde->bhe', kn, S)
            S = S + b_t[..., None, None] * kn[..., None] * (v_t - kp)[..., None, :]
            o = jnp.einsum('bhji,bhj->bhi', S, q_t)
            R = aR_t[..., None] * R
            kpR = jnp.einsum('bhd,bhde->bhe', kn, R)
            R = R + g_t[..., None, None] * kn[..., None] * (r - kpR)[..., None, :]
            o = o + jnp.einsum('bhji,bhj->bhi', R, q_t)
            return ((S, R), o)
        _, os = jax.lax.scan(step, (S0, S0), xs)
        out = jnp.moveaxis(os, 0, 1).reshape(Bs, Ts, DI) @ Wo.T
        return out + residual

    def _L0_ffn_ref(hidden_states, router_w, e_bias, Wg, Wu, Wd, SWg, SWu, SWd):
        import jax, jax.numpy as jnp
        import numpy as np
        H = 256
        I = 128
        E = 64
        G = 8
        TOPK_GROUP = 4
        K = 8
        I_SH = 256
        SCALE = 2.5

        def _route(x, router_w, e_bias):
            T = x.shape[0]
            scores = jax.nn.sigmoid(x.astype(jnp.float32) @ router_w.T.astype(jnp.float32))
            sfc = jax.lax.stop_gradient(scores) + e_bias[None, :]
            group_scores = jax.lax.top_k(sfc.reshape(T, G, E // G), 2)[0].sum(-1)
            _, gidx = jax.lax.top_k(group_scores, TOPK_GROUP)
            gmask = jax.nn.one_hot(gidx, G, dtype=sfc.dtype).sum(1)
            smask = jnp.repeat(gmask, E // G, axis=1)
            masked = jnp.where(smask > 0, sfc, 0.0)
            _, topk_idx = jax.lax.top_k(masked, K)
            w = jnp.take_along_axis(scores, topk_idx, axis=1)
            w = w / (w.sum(-1, keepdims=True) + 1e-20)
            return (topk_idx, w * SCALE)
        orig_shape = hidden_states.shape
        x = hidden_states.reshape(-1, orig_shape[-1])
        T = x.shape[0]
        topk_idx, topk_w = _route(x, router_w, e_bias)
        coef = jnp.zeros((T, E), topk_w.dtype).at[jnp.arange(T)[:, None], topk_idx].add(topk_w)
        g = jnp.einsum('th,ehi->tei', x, Wg)
        u = jnp.einsum('th,ehi->tei', x, Wu)
        h = jax.nn.silu(g) * u * coef[:, :, None]
        moe_out = jnp.einsum('tei,eih->th', h, Wd)
        shared = jax.nn.silu(x @ SWg) * (x @ SWu) @ SWd
        return (moe_out + shared).reshape(orig_shape)
    x = L0_attn_x
    x = x + _layernorm(_L0_attn_ref(_layernorm(x, axis=-1), L0_attn_Wq, L0_attn_Wk, L0_attn_Wv, L0_attn_Wa, L0_attn_ba, L0_attn_Wb, L0_attn_bb, L0_attn_Wg, L0_attn_bg, L0_attn_WaR, L0_attn_baR, L0_attn_Wo, L0_attn_ln_w, L0_attn_ln_b), axis=-1)
    x = x + _layernorm(_L0_ffn_ref(_layernorm(x, axis=-1), L0_ffn_router_w, L0_ffn_e_bias, L0_ffn_Wg, L0_ffn_Wu, L0_ffn_Wd, L0_ffn_SWg, L0_ffn_SWu, L0_ffn_SWd), axis=-1)
    return x

_drawn_inputs = setup_inputs


def setup_inputs(seed=0):
    import zlib

    import numpy as np

    out = dict(_drawn_inputs(seed))
    spreads = {'L0_attn_ba': (3.0, 0.2),
     'L0_attn_bb': (0.0, 0.1),
     'L0_attn_bg': (0.0, 0.1),
     'L0_attn_baR': (3.0, 0.2),
     'L0_attn_ln_w': (1.0, 0.2),
     'L0_attn_ln_b': (0.0, 0.1),
     'L0_ffn_e_bias': (0.0, 0.1)}
    factors = {}
    for name, (base, spread) in spreads.items():
        noise = np.random.default_rng([zlib.crc32(name.encode()), seed]).standard_normal(out[name].shape)
        drawn = base * np.exp(spread * noise) if base else spread * noise
        out[name] = jnp.asarray(drawn.astype(out[name].dtype))
    for name, factor in factors.items():
        out[name] = (out[name] * factor).astype(out[name].dtype)
    return out
```

```python
from contextlib import ExitStack

import concourse.bass as bass
from concourse import mybir

ALU = mybir.AluOpType
ACT = mybir.ActivationFunctionType
F32 = mybir.dt.float32
AX_X = mybir.AxisListType.X

P = 128
C = 64
NB = 6
Q = 32
LEVELS = 4
EPS = 1e-5
K_TINY = 1e-24
STREAMS = [(0, 0), (1, 0), (0, 1), (1, 1)]

JOBS = []
for _h in range(2):
    JOBS.append((f"V{_h}", "act"))
for _g in range(2):
    for _h in range(2):
        JOBS.append((f"KT{_g}{_h}", "act"))
for _g, _h in STREAMS:
    JOBS.append((f"A{_g}{_h}", "dve"))
for _i in range(4):
    JOBS.append((f"PQ{_i}", "dve"))
for _h in range(2):
    JOBS.append((f"RQ{_h}", "dve"))
for _l in range(1, LEVELS + 1):
    for _g in range(2):
        JOBS.append((f"Y{_l}{_g}", "dve"))
    for _g in range(2):
        JOBS.append((f"N{_l}{_g}", "act"))
for _g in range(2):
    JOBS.append((f"Z{_g}", "act"))
for _g in range(2):
    JOBS.append((f"X{_g}", "act"))
for _k, _e in (("KS", "dve"), ("KR", "dve"), ("U", "act"), ("PR", "dve"), ("W", "act"), ("O", "act"),
               ("SU", "dve"), ("RU", "dve")):
    for _h in range(2):
        JOBS.append((f"{_k}{_h}", _e))
JOBS.append(("OUT", "dve"))
JOB = {name: i for i, (name, _) in enumerate(JOBS)}
FRONT = [("SB", "dve"), ("XT", "act"), ("a0", "dve"), ("a1", "dve"), ("r0", "dve"), ("r1", "dve"),
         ("k0", "act"), ("k1", "act"), ("q0", "act"), ("q1", "act")]
FJOB = {name: i for i, (name, _) in enumerate(FRONT)}


def nth_of_engine(jobs, name):
    n = [j for j, _ in jobs].index(name)
    eng = jobs[n][1]
    return eng, sum(e == eng for _, e in jobs[:n + 1])


class Tensors:
    pass


def semaphores(nc, ctx, names):
    sems = {n: ctx.enter_context(nc.semaphore(n)) for n in names}
    return sems, [sems[n] for n in names]


def alloc_attention(nc, ctx):
    t = Tensors()

    def sb(name, shape):
        return ctx.enter_context(nc.sbuf_tensor(name, shape, F32))

    t.wq, t.wk, t.wa, t.war = (sb(n, [P, 2, 1024]) for n in ("wq", "wk", "wa", "war"))
    t.wv = sb("wv", [P, 2, 2, 512])
    t.wo = sb("wo", [P, 8, 256])
    t.wbg = sb("wbg", [P, 2, 2, 16])
    t.gate_bias = sb("gate_bias", [P, 2, 8])
    t.bg_bias = sb("bg_bias", [P, 2, 16])
    t.lnw, t.lnb = sb("lnw", [P, 2]), sb("lnb", [P, 2])
    t.ident = sb("ident", [P, P])
    t.eye = sb("eye", [P, C])
    t.strict = sb("strict", [P, C])
    t.pair_mask = sb("pair_mask", [P, Q])
    t.merge_mask = sb("merge_mask", [P, LEVELS, Q])
    t.pq_mask = sb("pq_mask", [P, 2, C])
    t.restart = sb("restart", [P, 1024])
    t.ones = sb("ones", [P, 1])

    t.S, t.R = sb("S", [P, 16, C]), sb("R", [P, 16, C])
    t.x_new, t.x_res, t.x2 = sb("x_new", [P, 256]), sb("x_res", [P, 256]), sb("x2", [P, 256])
    t.res, t.res_new = sb("res", [P, 256]), sb("res_new", [P, 256])
    t.xhat, t.y = sb("xhat", [P, 256]), sb("y", [P, 256])
    t.stats, t.mv, t.ln_tmp = sb("stats", [P, 3, 6]), sb("mv", [P, 3, 2]), sb("ln_tmp", [P, 3, 8])
    t.xnT = sb("xnT", [P, 2, P])
    t.z = sb("z", [P, 2, 1024])
    t.c = sb("c", [P, 2, 16, C])
    t.dec = sb("dec", [P, 2, 16, C + 1])
    t.dec_end = sb("dec_end", [P, 2, 16])
    t.k, t.q = sb("k", [P, 16, C]), sb("q", [P, 16, C])
    t.kplus = [sb("kplus_s", [P, 16, C]), sb("kplus_r", [P, 16, C])]
    t.kminus = [sb("kminus_s", [P, 16, C]), sb("kminus_r", [P, 16, C])]
    t.pq = sb("pq", [P, 2, 16, C])
    t.rqplus = sb("rqplus", [P, 16, C])
    t.V, t.bv = sb("V", [P, 16, C]), sb("bv", [P, 16, C])
    t.sc = sb("sc", [P, 8, 16])
    t.bgz = sb("bgz", [P, 2, 16])
    t.bg = sb("bg", [P, 2, 16])
    t.bn, t.nbn2 = sb("bn", [P, 2, 16]), sb("nbn2", [P, 2, 16])
    t.L = [sb("L_s", [P, 16, C]), sb("L_r", [P, 16, C])]
    t.T = [sb("T_s", [P, 16, Q]), sb("T_r", [P, 16, Q])]
    t.N = [sb("N_s", [P, 16, Q]), sb("N_r", [P, 16, Q])]
    t.Y = [sb("Y_s", [P, 16, Q]), sb("Y_r", [P, 16, Q])]
    t.inv = [sb("inv_s", [P, 16, C]), sb("inv_r", [P, 16, C])]
    t.pqT = sb("pqT", [P, 16, 2, C])
    t.rqT = sb("rqT", [P, 16, C])
    t.kT = [sb("kT_s", [P, 16, C]), sb("kT_r", [P, 16, C])]
    t.B, t.U, t.BR = sb("B", [P, 16, C]), sb("U", [P, 16, C]), sb("BR", [P, 16, C])
    t.ps = [ctx.enter_context(nc.psum_tensor(f"bank{i}", [P, 512], F32)) for i in range(8)]

    names = ["consts_loaded", "memset_done", "x_loaded", "x2_stored", "x_res_loaded",
             "mm_done", "front_mm", "dve_emptied", "act_emptied", "front_dve", "front_act",
             "dve_link", "act_link", "ln_var_ready", "ln_guess_ready", "xhat_ready", "x2_made", "dec_end_ready",
             "res_copied", "norm_sq_ready", "norm_guess_ready", "bg_z_ready", "bg_exp_ready",
             "scales_ready", "coef_ready", "L_ready", "T0_ready", "N0_ready", "T_ready", "inv_ready", "bv_ready", "B_ready", "BR_ready",
             "scan_done", "log_ready", "dec_ready", "plus_made", "sq_made", "u_vals", "states_ready", "pool_link"]
    t.sem, t.sems = semaphores(nc, ctx, names)
    return t


def empty_bank_wait(eng, t, jobs, name, front):
    who, n = nth_of_engine(jobs, name)
    if front:
        eng.wait_ge(t.sem["front_dve"] if who == "dve" else t.sem["front_act"], n)
    else:
        eng.wait_ge(t.sem["dve_emptied"] if who == "dve" else t.sem["act_emptied"], n)


def bc(ap, n):
    p, u = ap.shape
    return ap.rearrange("p (u o) -> p u o", o=1).broadcast_to([p, u, n])


def over(ap, u):
    p, n = ap.shape
    return ap.rearrange("p (o n) -> p o n", o=1).broadcast_to([p, u, n])


def blk(ap):
    return ap.rearrange("p (u n) -> p u n", n=C)


def chunk(nc, t, n, X, scratch, front):
    with nc.Block() as block:
        half = [slice(8 * h, 8 * h + 8) for h in range(2)]

        def bank(name):
            return t.ps[JOB[name] % NB]

        def fbank(name):
            return t.ps[NB + FJOB[name] % 2]

        @block.sync
        def _(sp):
            if front:
                for b in range(2):
                    sp.dma_start(t.x_new[C * b:C * b + C, :], X(n + 1, b)).then_inc(t.sem["x_loaded"], 16)
            sp.wait_ge(t.sem["x2_made"], 1)
            sp.dma_start(scratch(n), t.x2[:, :]).then_inc(t.sem["x2_stored"], 16)
            for b in range(2):
                sp.dma_start(t.x_res[C * b:C * b + C, :], X(n, b)).then_inc(t.sem["x_res_loaded"], 16)
            if front:
                sp.wait_ge(t.sem["x_loaded"], 32)
            sp.wait_ge(t.sem["x_res_loaded"], 32)
            sp.wait_ge(t.sem["x2_stored"], 16)

        @block.tensor
        def _(pe):
            def begin(name):
                q = JOB[name]
                if q >= NB:
                    empty_bank_wait(pe, t, JOBS, JOBS[q - NB][0], False)
                return bank(name)

            def units(name, h, pairs, last=True):
                ps = begin(name)
                for i, u in enumerate(range(8 * h, 8 * h + 8)):
                    for m, (lhsT, rhs) in enumerate(pairs):
                        for j in range(2):
                            r = slice(C * j, C * j + C)
                            mm = nc.tensor.matmul(ps[r, C * i:C * i + C], lhsT(r, u), rhs(r, u),
                                                  start=(m == 0), stop=(m == len(pairs) - 1))
                mm.then_inc(t.sem["mm_done"], 1)

            def of(x):
                return lambda r, u: x[r, u, :]

            def fbegin(name):
                q = FJOB[name]
                if q >= 2:
                    empty_bank_wait(pe, t, FRONT, FRONT[q - 2][0], True)
                return fbank(name)

            def projection(name, w, i):
                ps = fbegin(name)
                for m in range(4):
                    for kt in range(2):
                        hp = 4 * i + m
                        mm = nc.tensor.matmul(ps[:, P * m:P * m + P], w[:, kt, P * hp:P * hp + P],
                                              t.xnT[:, kt, :], start=(kt == 0), stop=(kt == 1))
                mm.then_inc(t.sem["front_mm"], 1)

            ps = fbegin("SB")
            for u in range(16):
                for j in range(2):
                    r = slice(C * j, C * j + C)
                    nc.tensor.matmul(ps[r, u:u + 1], t.BR[r, u, :], t.ones[r, :], start=True, stop=True)
            for b in range(2):
                for kt in range(2):
                    for j in range(2):
                        r = slice(C * j, C * j + C)
                        mm = nc.tensor.matmul(ps[r, 16 + b:48 + b:2], t.xnT[:, kt, C * b:C * b + C],
                                              t.wbg[:, kt, j, :], start=(kt == 0), stop=(kt == 1))
            mm.then_inc(t.sem["front_mm"], 1)
            for h in range(2):
                ps = begin(f"V{h}")
                for b in range(2):
                    for kt in range(2):
                        for j in range(2):
                            r = slice(C * j, C * j + C)
                            dst = ps[r, :].rearrange("p (m b d) -> p m b d", b=2, d=C)[:, :, b, :]
                            mm = nc.tensor.matmul(dst, t.xnT[:, kt, C * b:C * b + C],
                                                  t.wv[:, kt, j, 256 * h:256 * h + 256],
                                                  start=(kt == 0), stop=(kt == 1))
                mm.then_inc(t.sem["mm_done"], 1)
            for g in range(2):
                for h in range(2):
                    units(f"KT{g}{h}", h, [(of(t.kminus[g]), lambda r, u: t.eye[r, :])])
            for g, h in STREAMS:
                units(f"A{g}{h}", h, [(of(t.kplus[g]), of(t.kminus[g]))])
            for i in range(4):
                ps = begin(f"PQ{i}")
                for m in range(4):
                    u = 4 * i + m
                    for j in range(2):
                        r = slice(C * j, C * j + C)
                        mm = nc.tensor.matmul(ps[r, 2 * C * m:2 * C * m + 2 * C], t.kminus[0][r, u, :],
                                              t.pq[r, :, u, :], start=True, stop=True)
                mm.then_inc(t.sem["mm_done"], 1)
            for h in range(2):
                units(f"RQ{h}", h, [(of(t.kminus[1]), of(t.rqplus))])
            if front:
                pe.wait_ge(t.sem["xhat_ready"], 1)
                ps = fbegin("XT")
                for kt in range(2):
                    mm = nc.tensor.transpose(ps[:, P * kt:P * kt + P], t.xhat[:, P * kt:P * kt + P], t.ident[:, :])
                mm.then_inc(t.sem["front_mm"], 1)
            def blocks(name, lhsT, rhs):
                ps = begin(name)
                for u in range(16):
                    for q in range(4):
                        r = slice(Q * q, Q * q + Q)
                        mm = nc.tensor.matmul(ps[r, Q * u:Q * u + Q], lhsT(r, q, u), rhs[r, u, :], start=True, stop=True)
                mm.then_inc(t.sem["mm_done"], 1)

            for l in range(1, LEVELS + 1):
                if front:
                    if l == 1:
                        empty_bank_wait(pe, t, FRONT, "XT", True)
                    name, w = [("a", t.wa), ("r", t.war), ("k", t.wk), ("q", t.wq)][l - 1]
                for g in range(2):
                    if l == 1:
                        pe.wait_ge(t.sem["N0_ready"], g + 1)
                    else:
                        empty_bank_wait(pe, t, JOBS, f"N{l - 1}{g}", False)
                    blocks(f"Y{l}{g}", lambda r, q, u: t.L[g][r, u, Q * (q % 2):Q * (q % 2) + Q], t.N[g])
                    if front:
                        projection(f"{name}{g}", w, g)
                for g in range(2):
                    empty_bank_wait(pe, t, JOBS, f"Y{l}{g}", False)
                    if l > 1:
                        pe.wait_ge(t.sem["T_ready"], 2 * (l - 2) + g + 1)
                    blocks(f"N{l}{g}", lambda r, q, u: t.T[g][r, u, :], t.Y[g])
            for g in range(2):
                empty_bank_wait(pe, t, JOBS, f"N{LEVELS}{g}", False)
                ps = begin(f"Z{g}")
                for u in range(16):
                    for j in range(2):
                        top, low = slice(C * j, C * j + Q), slice(C * j + Q, C * j + C)
                        mm = nc.tensor.matmul(ps[top, Q * u:Q * u + Q], t.L[g][low, u, 0:Q], t.N[g][low, u, :],
                                              start=True, stop=True)
                mm.then_inc(t.sem["mm_done"], 1)
            for g in range(2):
                empty_bank_wait(pe, t, JOBS, f"Z{g}", False)
                pe.wait_ge(t.sem["T_ready"], 2 * (LEVELS - 1) + g + 1)
                ps = begin(f"X{g}")
                for u in range(16):
                    for j in range(2):
                        top = slice(C * j, C * j + Q)
                        mm = nc.tensor.matmul(ps[top, Q * u:Q * u + Q], t.T[g][top, u, :], t.Y[g][top, u, :],
                                              start=True, stop=True)
                mm.then_inc(t.sem["mm_done"], 1)
            for h in range(2):
                units(f"KS{h}", h, [(of(t.kplus[0]), of(t.S))])
            for h in range(2):
                units(f"KR{h}", h, [(of(t.kplus[1]), of(t.R))])
            for h in range(2):
                pe.wait_ge(t.sem["B_ready"], h + 1)
                empty_bank_wait(pe, t, JOBS, "X0", False)
                pe.wait_ge(t.sem["inv_ready"], 1)
                units(f"U{h}", h, [(of(t.inv[0]), of(t.B))])
            for h in range(2):
                empty_bank_wait(pe, t, JOBS, f"U{h}", False)
                units(f"PR{h}", h, [(lambda r, u: t.pq[r, 0, u, :], of(t.S)),
                                    (lambda r, u: t.pqT[r, u, 0, :], of(t.U))])
            for h in range(2):
                pe.wait_ge(t.sem["BR_ready"], h + 1)
                empty_bank_wait(pe, t, JOBS, "X1", False)
                pe.wait_ge(t.sem["inv_ready"], 2)
                units(f"W{h}", h, [(of(t.inv[1]), of(t.BR))])
            for h in range(2):
                empty_bank_wait(pe, t, JOBS, f"W{h}", False)
                units(f"O{h}", h, [(of(t.S), lambda r, u: t.pq[r, 1, u, :]),
                                   (of(t.U), lambda r, u: t.pqT[r, u, 1, :]),
                                   (of(t.R), of(t.rqplus)),
                                   (of(t.B), of(t.rqT))])
            for h in range(2):
                units(f"SU{h}", h, [(of(t.kT[0]), of(t.U))])
            for h in range(2):
                units(f"RU{h}", h, [(of(t.kT[1]), of(t.B))])
            ps = begin("OUT")
            for h in range(2):
                empty_bank_wait(pe, t, JOBS, f"O{h}", False)
            for hp in range(8):
                for b in range(2):
                    mm = nc.tensor.matmul(ps[C * b:C * b + C, 0:256], t.V[:, 2 * hp + b, :], t.wo[:, hp, :],
                                          start=(hp == 0), stop=(hp == 7))
            mm.then_inc(t.sem["mm_done"], 1)

        @block.vector
        def _(dve):
            links = [0]

            def link(ins):
                links[0] += 1
                ins.then_inc(t.sem["dve_link"], 1)
                dve.wait_ge(t.sem["dve_link"], links[0])

            def mm(name):
                dve.wait_ge(t.sem["mm_done"], JOB[name] + 1)
                return bank(name)

            def fmm(name):
                dve.wait_ge(t.sem["front_mm"], FJOB[name] + 1)
                return fbank(name)

            def ln_stats(i, src):
                link(nc.vector.bn_stats(t.stats[:, i, :], src))
                link(nc.vector.bn_aggr(t.mv[:, i, :], t.stats[:, i, :]))
                nc.vector.tensor_scalar(t.ln_tmp[:, i, 0:1], t.mv[:, i, 1:2], EPS, None,
                                        ALU.add).then_inc(t.sem["ln_var_ready"], 1)

            def ln_apply(i, order, dst, src):
                dve.wait_ge(t.sem["ln_guess_ready"], order)
                dve.wait_ge(t.sem["ln_var_ready"], order)
                v, r0 = t.ln_tmp[:, i, 0:1], t.ln_tmp[:, i, 2:3]
                link(nc.vector.tensor_scalar(t.ln_tmp[:, i, 3:4], v, r0, r0, ALU.mult, ALU.mult))
                link(nc.vector.tensor_scalar(t.ln_tmp[:, i, 4:5], t.ln_tmp[:, i, 3:4], -0.5, 1.5, ALU.mult, ALU.add))
                link(nc.vector.tensor_tensor(t.ln_tmp[:, i, 5:6], t.ln_tmp[:, i, 4:5], r0, ALU.mult))
                return nc.vector.tensor_scalar(dst, src, t.mv[:, i, 0:1], t.ln_tmp[:, i, 5:6],
                                               ALU.subtract, ALU.mult)

            nc.vector.tensor_copy(t.dec_end[:], t.dec[:, :, :, C]).then_inc(t.sem["dec_end_ready"], 1)
            ps = fmm("SB")
            nc.vector.tensor_scalar(t.sc[:, 0, :], ps[:, 0:16], K_TINY, None, ALU.max).then_inc(t.sem["norm_sq_ready"], 1)
            nc.vector.tensor_tensor(t.bgz[:], ps[:, 16:48].rearrange("p (g u) -> p g u", g=2), t.bg_bias[:],
                                    ALU.add).then_inc(t.sem["front_dve"], 1)
            ln_stats(2, t.y[:, :])
            dve.wait_ge(t.sem["norm_guess_ready"], 1)
            dve.wait_ge(t.sem["norm_sq_ready"], 1)
            link(nc.vector.tensor_tensor(t.sc[:, 3, :], t.sc[:, 0, :], t.sc[:, 2, :], ALU.mult))
            link(nc.vector.tensor_tensor(t.sc[:, 4, :], t.sc[:, 3, :], t.sc[:, 2, :], ALU.mult))
            link(nc.vector.tensor_scalar(t.sc[:, 5, :], t.sc[:, 4, :], -0.5, 1.5, ALU.mult, ALU.add))
            link(nc.vector.tensor_tensor(t.sc[:, 6, :], t.sc[:, 5, :], t.sc[:, 2, :], ALU.mult))
            dve.wait_ge(t.sem["bg_exp_ready"], 1)
            link(nc.vector.tensor_scalar(t.bg[:], t.bgz[:], 1.0, None, ALU.add))
            link(nc.vector.reciprocal(t.bg[:], t.bg[:]))
            nrm2 = over(t.sc[:, 6, :], 2)
            link(nc.vector.tensor_tensor(t.bn[:], t.bg[:], nrm2, ALU.mult))
            nc.vector.scalar_tensor_tensor(out=t.nbn2[:], in0=t.bn[:], scalar=-1.0, in1=nrm2,
                                           op0=ALU.mult, op1=ALU.mult).then_inc(t.sem["scales_ready"], 1)
            link(ln_apply(2, 1, t.y[:, :], t.y[:, :]))
            nc.vector.tensor_tensor(t.x2[:], t.x_res[:], t.y[:], ALU.add).then_inc(t.sem["x2_made"], 1)
            if front:
                dve.wait_ge(t.sem["x_loaded"], 32)
                ln_stats(0, t.x_new[:, :])
            for s, (g, h) in enumerate(STREAMS):
                ps = mm(f"A{g}{h}")
                dve.wait_ge(t.sem["coef_ready"], s + 1)
                nc.vector.tensor_tensor(t.L[g][:, half[h], :], blk(ps[:, :]), t.L[g][:, half[h], :],
                                        ALU.mult).then_inc(t.sem["dve_emptied"], 1)
                if s == 1 and front:
                    dve.wait_ge(t.sem["res_copied"], 1)
                    link(ln_apply(0, 2, t.res_new[:, :], t.x_new[:, :]))
                    ln_stats(1, t.res_new[:, :])
            if front:
                ln_apply(1, 3, t.xhat[:, :], t.res_new[:, :]).then_inc(t.sem["xhat_ready"], 1)
            for i in range(4):
                ps = mm(f"PQ{i}")
                nc.vector.tensor_tensor(t.pqT[:, 4 * i:4 * i + 4, :, :].rearrange("p u g n -> p u (g n)"),
                                        ps[:, :].rearrange("p (u n) -> p u n", n=2 * C),
                                        over(t.pq_mask[:].rearrange("p g n -> p (g n)"), 4),
                                        ALU.mult).then_inc(t.sem["dve_emptied"], 1)
            for h in range(2):
                ps = mm(f"RQ{h}")
                nc.vector.tensor_tensor(t.rqT[:, half[h], :], blk(ps[:, :]), over(t.pq_mask[:, 1, :], 8),
                                        ALU.mult).then_inc(t.sem["dve_emptied"], 1)

            def add_gate_bias(gate, i):
                ps = fmm(f"{'ar'[gate]}{i}")
                nc.vector.tensor_tensor(
                    t.z[:, gate, 512 * i:512 * i + 512].rearrange("p (m n) -> p m n", n=P),
                    ps[:, :].rearrange("p (m n) -> p m n", n=P),
                    bc(t.gate_bias[:, gate, 4 * i:4 * i + 4], P), ALU.add).then_inc(t.sem["front_dve"], 1)

            def running_sum(gate):
                dve.wait_ge(t.sem["log_ready"], gate + 1)
                nc.vector.tensor_tensor_scan(t.c[:, gate, :, :].rearrange("p u n -> p (u n)"), t.restart[:],
                                             t.z[:, gate, :], 0.0, ALU.mult, ALU.add).then_inc(t.sem["scan_done"], 1)

            for g in range(2):
                dve.wait_ge(t.sem["T0_ready"], g + 1)
                nc.vector.transpose(t.N[g][:], t.T[g][:]).then_inc(t.sem["N0_ready"], 1)
            for l in range(1, LEVELS + 1):
                for g in range(2):
                    ps = mm(f"Y{l}{g}")
                    nc.vector.tensor_tensor(t.Y[g][:], ps[:, :].rearrange("p (u n) -> p u n", n=Q),
                                            over(t.merge_mask[:, l - 1, :], 16), ALU.mult).then_inc(t.sem["dve_emptied"], 1)
                    if front and l <= 2:
                        add_gate_bias(l - 1, g)
                for g in range(2):
                    empty_bank_wait(dve, t, JOBS, f"N{l}{g}", False)
                    nc.vector.transpose(t.T[g][:], t.N[g][:]).then_inc(t.sem["T_ready"], 1)
                if front and l >= 3:
                    running_sum(l - 3)
            for h in range(2):
                ps = mm(f"KS{h}")
                link(nc.vector.tensor_tensor(t.B[:, half[h], :], blk(ps[:, :]), bc(t.nbn2[:, 0, half[h]], C),
                                             ALU.mult))
                dve.wait_ge(t.sem["bv_ready"], 1)
                nc.vector.tensor_tensor(t.B[:, half[h], :], t.B[:, half[h], :], t.bv[:, half[h], :],
                                        ALU.add).then_inc(t.sem["B_ready"], 1)
                dve.wait_ge(t.sem["B_ready"], h + 1)
                dve.sem_inc(t.sem["dve_emptied"], 1)
            for h in range(2):
                ps = mm(f"KR{h}")
                nc.vector.tensor_tensor(t.BR[:, half[h], :], blk(ps[:, :]), bc(t.nbn2[:, 1, half[h]], C),
                                        ALU.mult).then_inc(t.sem["dve_emptied"], 1)
            for h in range(2):
                ps = mm(f"PR{h}")
                r = t.bv[:, half[h], :]
                nc.vector.tensor_tensor(r, blk(ps[:, :]), bc(t.sc[:, 6, half[h]], C), ALU.mult).then_inc(t.sem["dve_emptied"], 1)
                empty_bank_wait(dve, t, JOBS, f"PR{h}", False)
                link(nc.vector.tensor_tensor(r, t.V[:, half[h], :], r, ALU.subtract))
                link(nc.vector.tensor_scalar(r, r, -1.0, 1.0, ALU.max, ALU.min))
                link(nc.vector.tensor_tensor(r, r, bc(t.bn[:, 1, half[h]], C), ALU.mult))
                nc.vector.tensor_tensor(t.BR[:, half[h], :], t.BR[:, half[h], :], r, ALU.add).then_inc(t.sem["BR_ready"], 1)
            for g, state in enumerate((t.S, t.R)):
                for h in range(2):
                    ps = mm(f"{'SR'[g]}U{h}")
                    nc.vector.tensor_tensor(state[:, half[h], :], blk(ps[:, :]), state[:, half[h], :],
                                            ALU.add).then_inc(t.sem["dve_emptied"], 1)
                    empty_bank_wait(dve, t, JOBS, f"{'SR'[g]}U{h}", False)
                    nc.vector.tensor_tensor(state[:, half[h], :], state[:, half[h], :],
                                            bc(t.dec_end[:, g, half[h]], C), ALU.mult).then_inc(t.sem["states_ready"], 1)
            ps = mm("OUT")
            dve.wait_ge(t.sem["res_copied"], 1)
            nc.vector.tensor_tensor(t.y[:], ps[:, 0:256], t.res[:], ALU.add).then_inc(t.sem["dve_emptied"], 1)

        @block.scalar
        def _(act):
            links = [0]

            def link(ins):
                links[0] += 1
                ins.then_inc(t.sem["act_link"], 1)
                act.wait_ge(t.sem["act_link"], links[0])

            def empty(name, dst):
                act.wait_ge(t.sem["mm_done"], JOB[name] + 1)
                nc.scalar.copy(dst, blk(bank(name)[:, :])).then_inc(t.sem["act_emptied"], 1)

            def ln_guess(i, order):
                act.wait_ge(t.sem["ln_var_ready"], order)
                link(nc.scalar.activation(t.ln_tmp[:, i, 1:2], t.ln_tmp[:, i, 0:1], ACT.Ln))
                nc.scalar.activation(t.ln_tmp[:, i, 2:3], t.ln_tmp[:, i, 1:2], ACT.Exp,
                                     scale=-0.5).then_inc(t.sem["ln_guess_ready"], 1)

            act.wait_ge(t.sem["norm_sq_ready"], 1)
            link(nc.scalar.activation(t.sc[:, 1, :], t.sc[:, 0, :], ACT.Ln))
            nc.scalar.activation(t.sc[:, 2, :], t.sc[:, 1, :], ACT.Exp, scale=-0.5).then_inc(t.sem["norm_guess_ready"], 1)
            empty_bank_wait(act, t, FRONT, "SB", True)
            nc.scalar.activation(t.bgz[:], t.bgz[:], ACT.Exp, scale=-1.0).then_inc(t.sem["bg_exp_ready"], 1)
            ln_guess(2, 1)
            for h in range(2):
                empty(f"V{h}", t.V[:, half[h], :])
            for g in range(2):
                for h in range(2):
                    empty(f"KT{g}{h}", t.kT[g][:, half[h], :])
            if front:
                ln_guess(0, 2)
                ln_guess(1, 3)
                act.wait_ge(t.sem["front_mm"], FJOB["XT"] + 1)
                ps = fbank("XT")
                for kt in range(2):
                    ins = nc.scalar.activation(t.xnT[:, kt, :], ps[:, P * kt:P * kt + P], ACT.Identity,
                                               bias=t.lnb[:, kt:kt + 1], scale=t.lnw[:, kt:kt + 1])
                ins.then_inc(t.sem["front_act"], 1)
            def exp_gate(gate):
                empty_bank_wait(act, t, FRONT, f"{'ar'[gate]}1", True)
                link(nc.scalar.activation(t.z[:, gate, :], t.z[:, gate, :], ACT.Exp, scale=-1.0))
                nc.scalar.activation(t.z[:, gate, :], t.z[:, gate, :], ACT.Ln, bias=1.0).then_inc(t.sem["log_ready"], 1)

            def decays(gate):
                act.wait_ge(t.sem["scan_done"], gate + 1)
                act.wait_ge(t.sem["dec_end_ready"], 1)
                link(nc.scalar.activation(t.dec[:, gate, :, 1:C + 1], t.c[:, gate, :, :], ACT.Exp, scale=-1.0))
                nc.scalar.activation(t.c[:, gate, :, :], t.c[:, gate, :, :], ACT.Exp).then_inc(t.sem["dec_ready"], 1)

            def front_copy(name, dst):
                act.wait_ge(t.sem["front_mm"], FJOB[name] + 1)
                nc.scalar.copy(dst, blk(fbank(name)[:, :])).then_inc(t.sem["front_act"], 1)

            for l in range(1, LEVELS + 1):
                for g in range(2):
                    act.wait_ge(t.sem["mm_done"], JOB[f"N{l}{g}"] + 1)
                    nc.scalar.copy(t.N[g][:], bank(f"N{l}{g}")[:, :].rearrange("p (u n) -> p u n", n=Q)).then_inc(
                        t.sem["act_emptied"], 1)
                if front and l in (1, 2):
                    exp_gate(l - 1)
                if front and l == 3:
                    front_copy("k0", t.k[:, half[0], :])
                    front_copy("k1", t.k[:, half[1], :])
                    decays(0)
                if front and l == 4:
                    front_copy("q0", t.q[:, half[0], :])
                    front_copy("q1", t.q[:, half[1], :])
            for k, dst, off in (("Z", t.Y, 0), ("X", t.inv, Q)):
                for g in range(2):
                    act.wait_ge(t.sem["mm_done"], JOB[f"{k}{g}"] + 1)
                    for j in range(2):
                        r = slice(C * j, C * j + Q)
                        ins = nc.scalar.copy(dst[g][r, :, off:off + Q],
                                             bank(f"{k}{g}")[r, :].rearrange("p (u n) -> p u n", n=Q))
                    ins.then_inc(t.sem["act_emptied"], 1)
                if front and k == "Z":
                    decays(1)
            for h in range(2):
                empty(f"U{h}", t.U[:, half[h], :])
            for h in range(2):
                empty(f"W{h}", t.B[:, half[h], :])
            for h in range(2):
                empty(f"O{h}", t.V[:, half[h], :])

        @block.gpsimd
        def _(pool):
            nc.gpsimd.tensor_copy(t.res[:], t.res_new[:]).then_inc(t.sem["res_copied"], 1)
            pool.wait_ge(t.sem["scales_ready"], 1)
            for g, h in STREAMS:
                nc.gpsimd.tensor_tensor(t.L[g][:, half[h], :], bc(t.nbn2[:, g, half[h]], C), over(t.strict[:], 8),
                                        ALU.mult).then_inc(t.sem["coef_ready"], 1)
            empty_bank_wait(pool, t, JOBS, "V1", False)
            nc.gpsimd.tensor_tensor(t.bv[:], t.V[:], bc(t.bn[:, 0, :], C), ALU.mult).then_inc(t.sem["bv_ready"], 1)
            for s, (g, h) in enumerate(STREAMS):
                empty_bank_wait(pool, t, JOBS, f"A{g}{h}", False)
                nc.gpsimd.tensor_tensor(t.L[g][:, half[h], :], t.L[g][:, half[h], :], over(t.eye[:], 8),
                                        ALU.add).then_inc(t.sem["L_ready"], 1)
            pool.wait_ge(t.sem["L_ready"], 4)
            for g in range(2):
                for q in range(4):
                    r = slice(Q * q, Q * q + Q)
                    ins = nc.gpsimd.tensor_tensor(t.T[g][r, :, :], t.L[g][r, :, Q * (q % 2):Q * (q % 2) + Q],
                                                  over(t.pair_mask[r, :], 16), ALU.mult)
                ins.then_inc(t.sem["T0_ready"], 1)
            for g in range(2):
                empty_bank_wait(pool, t, JOBS, f"N{LEVELS}{g}", False)
                for q in range(4):
                    r = slice(Q * q, Q * q + Q)
                    ins = nc.gpsimd.tensor_copy(t.inv[g][r, :, Q * (q % 2):Q * (q % 2) + Q], t.N[g][r, :, :])
                ins.then_inc(t.sem["inv_ready"], 1)
            pool.wait_ge(t.sem["inv_ready"], 2)
            if front:
                def product(last_use, dst, a, b):
                    pool.wait_ge(t.sem["mm_done"], JOB[last_use] + 1)
                    nc.gpsimd.tensor_tensor(dst, a, b, ALU.mult).then_inc(t.sem["plus_made"], 1)

                empty_bank_wait(pool, t, FRONT, "k1", True)
                for g in range(2):
                    pool.wait_ge(t.sem["dec_ready"], g + 1)
                    product("RQ1", t.kminus[g][:], t.k[:], t.c[:, g, :, :])
                product("KS1", t.kplus[0][:], t.k[:], t.dec[:, 0, :, 1:C + 1])
                product("KR1", t.kplus[1][:], t.k[:], t.dec[:, 1, :, 1:C + 1])
                product("PR1", t.pq[:, 0, :, :], t.k[:], t.dec[:, 0, :, 0:C])
                product("W1", t.BR[:], t.k[:], t.k[:])
                empty_bank_wait(pool, t, FRONT, "q1", True)
                product("O1", t.pq[:, 1, :, :], t.q[:], t.dec[:, 0, :, 1:C + 1])
                product("O1", t.rqplus[:], t.q[:], t.dec[:, 1, :, 1:C + 1])


def first_front(nc, t, X, consts):
    with nc.Block() as block:
        half = [slice(8 * h, 8 * h + 8) for h in range(2)]

        @block.sync
        def _(sp):
            for b in range(2):
                sp.dma_start(t.x_new[C * b:C * b + C, :], X(0, b)).then_inc(t.sem["x_loaded"], 16)
            for dst, src in consts:
                sp.dma_start(dst, src).then_inc(t.sem["consts_loaded"], 16)
            sp.wait_ge(t.sem["consts_loaded"], 16 * len(consts))

        @block.gpsimd
        def _(pool):
            nc.gpsimd.memset(t.S[:], 0.0)
            nc.gpsimd.memset(t.R[:], 0.0)
            nc.gpsimd.memset(t.y[:], 0.0)
            nc.gpsimd.memset(t.x_res[:], 0.0)
            nc.gpsimd.memset(t.ones[:], 1.0)
            nc.gpsimd.memset(t.inv[0][:], 0.0)
            nc.gpsimd.memset(t.inv[1][:], 0.0)
            nc.gpsimd.memset(t.dec[:, :, :, 0:1], 1.0).then_inc(t.sem["memset_done"], 1)
            pool.wait_ge(t.sem["memset_done"], 1)
            for g in range(2):
                pool.wait_ge(t.sem["dec_ready"], g + 1)
                nc.gpsimd.tensor_tensor(t.kminus[g][:], t.k[:], t.c[:, g, :, :], ALU.mult)
                nc.gpsimd.tensor_tensor(t.kplus[g][:], t.k[:], t.dec[:, g, :, 1:C + 1], ALU.mult)
            nc.gpsimd.tensor_tensor(t.pq[:, 0, :, :], t.k[:], t.dec[:, 0, :, 0:C], ALU.mult)
            nc.gpsimd.tensor_tensor(t.BR[:], t.k[:], t.k[:], ALU.mult)
            nc.gpsimd.tensor_tensor(t.pq[:, 1, :, :], t.q[:], t.dec[:, 0, :, 1:C + 1], ALU.mult)
            nc.gpsimd.tensor_tensor(t.rqplus[:], t.q[:], t.dec[:, 1, :, 1:C + 1], ALU.mult)

        @block.vector
        def _(dve):
            links = [0]

            def link(ins):
                links[0] += 1
                ins.then_inc(t.sem["dve_link"], 1)
                dve.wait_ge(t.sem["dve_link"], links[0])

            dve.wait_ge(t.sem["x_loaded"], 32)
            for i, (src, dst) in enumerate(((t.x_new, t.res_new), (t.res_new, t.xhat))):
                link(nc.vector.bn_stats(t.stats[:, i, :], src[:, :]))
                link(nc.vector.bn_aggr(t.mv[:, i, :], t.stats[:, i, :]))
                nc.vector.tensor_scalar(t.ln_tmp[:, i, 0:1], t.mv[:, i, 1:2], EPS, None,
                                        ALU.add).then_inc(t.sem["ln_var_ready"], 1)
                dve.wait_ge(t.sem["ln_guess_ready"], i + 1)
                dve.wait_ge(t.sem["ln_var_ready"], i + 1)
                v, r0 = t.ln_tmp[:, i, 0:1], t.ln_tmp[:, i, 2:3]
                link(nc.vector.tensor_scalar(t.ln_tmp[:, i, 3:4], v, r0, r0, ALU.mult, ALU.mult))
                link(nc.vector.tensor_scalar(t.ln_tmp[:, i, 4:5], t.ln_tmp[:, i, 3:4], -0.5, 1.5, ALU.mult, ALU.add))
                link(nc.vector.tensor_tensor(t.ln_tmp[:, i, 5:6], t.ln_tmp[:, i, 4:5], r0, ALU.mult))
                ins = nc.vector.tensor_scalar(dst[:, :], src[:, :], t.mv[:, i, 0:1], t.ln_tmp[:, i, 5:6],
                                              ALU.subtract, ALU.mult)
                if i == 0:
                    link(ins)
                else:
                    ins.then_inc(t.sem["xhat_ready"], 1)
            dve.wait_ge(t.sem["consts_loaded"], 16 * len(consts))
            for gate in range(2):
                for i in range(2):
                    name = f"{'ar'[gate]}{i}"
                    dve.wait_ge(t.sem["front_mm"], 1 + 2 * gate + i + 1)
                    nc.vector.tensor_tensor(
                        t.z[:, gate, 512 * i:512 * i + 512].rearrange("p (m n) -> p m n", n=P),
                        t.ps[2 * gate + i][:, :].rearrange("p (m n) -> p m n", n=P),
                        bc(t.gate_bias[:, gate, 4 * i:4 * i + 4], P), ALU.add).then_inc(t.sem["front_dve"], 1)
            for gate in range(2):
                dve.wait_ge(t.sem["log_ready"], gate + 1)
                nc.vector.tensor_tensor_scan(t.c[:, gate, :, :].rearrange("p u n -> p (u n)"), t.restart[:],
                                             t.z[:, gate, :], 0.0, ALU.mult, ALU.add).then_inc(t.sem["scan_done"], 1)

        @block.tensor
        def _(pe):
            pe.wait_ge(t.sem["consts_loaded"], 16 * len(consts))
            pe.wait_ge(t.sem["xhat_ready"], 1)
            for kt in range(2):
                mm = nc.tensor.transpose(t.ps[6][:, P * kt:P * kt + P], t.xhat[:, P * kt:P * kt + P], t.ident[:, :])
            mm.then_inc(t.sem["front_mm"], 1)
            pe.wait_ge(t.sem["front_act"], 1)
            for f, w in enumerate((t.wa, t.war, t.wk)):
                for i in range(2):
                    for m in range(4):
                        for kt in range(2):
                            hp = 4 * i + m
                            mm = nc.tensor.matmul(t.ps[2 * f + i][:, P * m:P * m + P], w[:, kt, P * hp:P * hp + P],
                                                  t.xnT[:, kt, :], start=(kt == 0), stop=(kt == 1))
                    mm.then_inc(t.sem["front_mm"], 1)
            for i in range(2):
                for m in range(4):
                    for kt in range(2):
                        hp = 4 * i + m
                        mm = nc.tensor.matmul(t.ps[6 + i][:, P * m:P * m + P], t.wq[:, kt, P * hp:P * hp + P],
                                              t.xnT[:, kt, :], start=(kt == 0), stop=(kt == 1))
                mm.then_inc(t.sem["front_mm"], 1)

        @block.scalar
        def _(act):
            links = [0]

            def link(ins):
                links[0] += 1
                ins.then_inc(t.sem["act_link"], 1)
                act.wait_ge(t.sem["act_link"], links[0])

            nc.scalar.preload_act_table_set("natural_log_exp_and_others")
            for i in range(2):
                act.wait_ge(t.sem["ln_var_ready"], i + 1)
                link(nc.scalar.activation(t.ln_tmp[:, i, 1:2], t.ln_tmp[:, i, 0:1], ACT.Ln))
                nc.scalar.activation(t.ln_tmp[:, i, 2:3], t.ln_tmp[:, i, 1:2], ACT.Exp,
                                     scale=-0.5).then_inc(t.sem["ln_guess_ready"], 1)
            act.wait_ge(t.sem["consts_loaded"], 16 * len(consts))
            act.wait_ge(t.sem["front_mm"], 1)
            for kt in range(2):
                ins = nc.scalar.activation(t.xnT[:, kt, :], t.ps[6][:, P * kt:P * kt + P], ACT.Identity,
                                           bias=t.lnb[:, kt:kt + 1], scale=t.lnw[:, kt:kt + 1])
            ins.then_inc(t.sem["front_act"], 1)
            for gate in range(2):
                act.wait_ge(t.sem["front_dve"], 2 * gate + 2)
                link(nc.scalar.activation(t.z[:, gate, :], t.z[:, gate, :], ACT.Exp, scale=-1.0))
                nc.scalar.activation(t.z[:, gate, :], t.z[:, gate, :], ACT.Ln, bias=1.0).then_inc(t.sem["log_ready"], 1)
            for h in range(2):
                act.wait_ge(t.sem["front_mm"], 5 + h + 1)
                nc.scalar.copy(t.k[:, half[h], :], blk(t.ps[4 + h][:, :]))
            for h in range(2):
                act.wait_ge(t.sem["front_mm"], 7 + h + 1)
                ins = nc.scalar.copy(t.q[:, half[h], :], blk(t.ps[6 + h][:, :]))
            for gate in range(2):
                act.wait_ge(t.sem["scan_done"], gate + 1)
                act.wait_ge(t.sem["memset_done"], 1)
                link(nc.scalar.activation(t.dec[:, gate, :, 1:C + 1], t.c[:, gate, :, :], ACT.Exp, scale=-1.0))
                nc.scalar.activation(t.c[:, gate, :, :], t.c[:, gate, :, :], ACT.Exp).then_inc(t.sem["dec_ready"], 1)


def last_layernorm(nc, t, scratch_slot):
    with nc.Block() as block:
        @block.vector
        def _(dve):
            links = [0]

            def link(ins):
                links[0] += 1
                ins.then_inc(t.sem["dve_link"], 1)
                dve.wait_ge(t.sem["dve_link"], links[0])

            link(nc.vector.bn_stats(t.stats[:, 2, :], t.y[:, :]))
            link(nc.vector.bn_aggr(t.mv[:, 2, :], t.stats[:, 2, :]))
            nc.vector.tensor_scalar(t.ln_tmp[:, 2, 0:1], t.mv[:, 2, 1:2], EPS, None,
                                    ALU.add).then_inc(t.sem["ln_var_ready"], 1)
            dve.wait_ge(t.sem["ln_guess_ready"], 1)
            dve.wait_ge(t.sem["ln_var_ready"], 1)
            v, r0 = t.ln_tmp[:, 2, 0:1], t.ln_tmp[:, 2, 2:3]
            link(nc.vector.tensor_scalar(t.ln_tmp[:, 2, 3:4], v, r0, r0, ALU.mult, ALU.mult))
            link(nc.vector.tensor_scalar(t.ln_tmp[:, 2, 4:5], t.ln_tmp[:, 2, 3:4], -0.5, 1.5, ALU.mult, ALU.add))
            link(nc.vector.tensor_tensor(t.ln_tmp[:, 2, 5:6], t.ln_tmp[:, 2, 4:5], r0, ALU.mult))
            link(nc.vector.tensor_scalar(t.y[:, :], t.y[:, :], t.mv[:, 2, 0:1], t.ln_tmp[:, 2, 5:6],
                                         ALU.subtract, ALU.mult))
            nc.vector.tensor_tensor(t.x2[:], t.x_res[:], t.y[:], ALU.add).then_inc(t.sem["x2_made"], 1)

        @block.scalar
        def _(act):
            act.wait_ge(t.sem["ln_var_ready"], 1)
            nc.scalar.activation(t.ln_tmp[:, 2, 1:2], t.ln_tmp[:, 2, 0:1], ACT.Ln).then_inc(t.sem["act_link"], 1)
            act.wait_ge(t.sem["act_link"], 1)
            nc.scalar.activation(t.ln_tmp[:, 2, 2:3], t.ln_tmp[:, 2, 1:2], ACT.Exp,
                                 scale=-0.5).then_inc(t.sem["ln_guess_ready"], 1)

        @block.sync
        def _(sp):
            sp.wait_ge(t.sem["x2_made"], 1)
            sp.dma_start(scratch_slot, t.x2[:, :]).then_inc(t.sem["x2_stored"], 16)
            sp.wait_ge(t.sem["x2_stored"], 16)


def clear(nc, sems):
    nc.gpsimd.sem_clear(range(sems[0].num, sems[-1].num + 1))
    nc.all_engine_barrier()


def attention_stage(nc, a, scratch):
    B, T, D = a["x"].shape
    chunks = T // C
    Xv = a["x"].rearrange("b (n t) d -> n b t d", t=C)
    with ExitStack() as ctx:
        t = alloc_attention(nc, ctx)

        def X(n, b):
            if isinstance(n, int):
                return Xv[n, b]
            return Xv[bass.ds(n, 1), b].rearrange("o t d -> (o t) d")

        def slot(n):
            if isinstance(n, int):
                return scratch[n]
            return scratch[bass.ds(n, 1)].rearrange("o p d -> (o p) d")

        consts = [(t.lnw[:], a["lnw"]), (t.lnb[:], a["lnb"]), (t.ident[:], a["ident"]), (t.wa[:], a["wa"]),
                  (t.gate_bias[:], a["gate_bias"]), (t.war[:], a["war"]), (t.wk[:], a["wk"]), (t.wq[:], a["wq"]),
                  (t.restart[:], a["restart"]),
                  (t.wv[:], a["wv"]), (t.wo[:], a["wo"]), (t.wbg[:], a["wbg"]), (t.bg_bias[:], a["bg_bias"]),
                  (t.eye[:], a["eye"]), (t.strict[:], a["strict"]), (t.pair_mask[:], a["pair_mask"]),
                  (t.merge_mask[:], a["merge_mask"]), (t.pq_mask[:], a["pq_mask"])]
        first_front(nc, t, X, consts)
        clear(nc, t.sems)
        with nc.Fori(0, chunks - 1) as n:
            chunk(nc, t, n, X, slot, True)
            clear(nc, t.sems)
        chunk(nc, t, chunks - 1, X, slot, False)
        clear(nc, t.sems)
        last_layernorm(nc, t, scratch[chunks])
        clear(nc, t.sems)



E = 64
G = 8
TOP = 8
SCALE = 2.5
BIG = 3.0e38
TILES = 32
BLOCKS = 8


def moe_stage(nc, a, scratch, out):
    H = 256
    with ExitStack() as ctx:
        def sb(name, shape):
            return ctx.enter_context(nc.sbuf_tensor(name, shape, F32))

        x2 = sb("x2_all", [P, TILES, H])
        acc = sb("acc", [P, TILES, H])
        xfT = sb("xfT", [P, 2, TILES * P])
        coef = sb("coef", [P, TILES, E + 2])
        coef_e = sb("coef_e", [P, 2, TILES])
        ident = sb("ident_b", [P, P])
        rw = sb("rw", [P, 2, E])
        e_bias = sb("e_bias", [P, E])
        wg, wu = sb("wg", [P, 2, 2, P]), sb("wu", [P, 2, 2, P])
        wd = sb("wd", [P, 2, H])
        stats, mv, var = sb("stats_b", [P, TILES, 6]), sb("mv_b", [P, TILES, 2]), sb("var_b", [P, TILES])
        lnv, r0, nt, rstd = (sb(n, [P, TILES]) for n in ("lnv", "r0", "nt", "rstd"))
        xf = sb("xf", [P, 4, H])
        xfs = sb("xfs", [P, 2, 4 * P])
        score, sfc, work = sb("score", [P, 4, E]), sb("sfc", [P, 4, E]), sb("work", [P, 4, E])
        top = sb("top", [P, 4, G, 8])
        gsum, gtop, grep, gmask = (sb(n, [P, 4, 8]) for n in ("gsum", "gtop", "grep_", "gmask"))
        wsum, winv = sb("wsum", [P, 4]), sb("winv", [P, 4])
        sg, h = sb("sg", [P, 2, 512]), sb("h", [P, 2, 512])
        ps = [ctx.enter_context(nc.psum_tensor(f"bank_b{i}", [P, 512], F32)) for i in range(8)]

        names = ["loaded", "cleared", "link", "var_ready", "guess_ready", "xf_ready", "xfT_done", "xfT_copied",
                 "logits_done", "exp_ready", "xfT_kept", "weights_loaded", "next_loaded", "coef_ready", "gu_done", "silu_done",
                 "h_done", "y_done", "y_added", "stored", "a_link", "rows_ready"]
        s, sems = semaphores(nc, ctx, names)

        with nc.Block() as block:
            @block.sync
            def _(sp):
                for i in range(4):
                    sp.dma_start(x2[:, 8 * i:8 * i + 8, :],
                                 scratch[1 + 8 * i:9 + 8 * i].rearrange("n p d -> p n d")).then_inc(s["loaded"], 16)
                sp.dma_start(ident[:], a["ident"]).then_inc(s["stored"], 16)
                sp.dma_start(rw[:], a["rw"]).then_inc(s["stored"], 16)
                sp.dma_start(e_bias[:], a["e_bias"]).then_inc(s["stored"], 16)
                load_expert(sp, a, wg, wu, wd, 0, 0, s["stored"])
                sp.wait_ge(s["loaded"], 64)
                sp.wait_ge(s["stored"], 16 * 6)

            @block.gpsimd
            def _(pool):
                nc.gpsimd.memset(acc[:], 0.0)
                nc.gpsimd.memset(coef[:, :, E:E + 2], 1.0).then_inc(s["cleared"], 1)
                pool.wait_ge(s["cleared"], 1)

            @block.vector
            def _(dve):
                dve.wait_ge(s["loaded"], 64)
                for i in range(TILES):
                    nc.vector.bn_stats(stats[:, i, :], x2[:, i, :]).then_inc(s["link"], 1)
                for i in range(TILES):
                    dve.wait_ge(s["link"], i + 1)
                    nc.vector.bn_aggr(mv[:, i, :], stats[:, i, :]).then_inc(s["link"], 1)
                rsqrt_vector(nc, dve, s, mv, var, r0, nt, rstd, 2 * TILES)

            @block.scalar
            def _(act):
                rsqrt_scalar(nc, act, s, var, lnv, r0)

        clear(nc, sems)
        with nc.Fori(0, BLOCKS) as i:
            route_block(nc, s, i, x2, xfT, coef, ident, rw, e_bias, mv, rstd, xf, xfs, score, sfc, work, top, gsum,
                        gtop, grep, gmask, wsum, winv, ps)
            clear(nc, sems)
        with nc.Fori(0, E // 2) as i:
            expert_pair(nc, s, a, i, True, wg, wu, wd, coef, coef_e, xfT, sg, h, acc, ps)
            clear(nc, sems)
        expert_pair(nc, s, a, E // 2, False, wg, wu, wd, coef, coef_e, xfT, sg, h, acc, ps)
        clear(nc, sems)

        Ov = out.rearrange("b (n t) d -> b t n d", t=C)
        with nc.Block() as block:
            @block.vector
            def _(dve):
                for i in range(TILES):
                    nc.vector.bn_stats(stats[:, i, :], acc[:, i, :]).then_inc(s["link"], 1)
                for i in range(TILES):
                    dve.wait_ge(s["link"], i + 1)
                    nc.vector.bn_aggr(mv[:, i, :], stats[:, i, :]).then_inc(s["link"], 1)
                rsqrt_vector(nc, dve, s, mv, var, r0, nt, rstd, 2 * TILES)
                dve.wait_ge(s["rows_ready"], 1)
                for i in range(TILES):
                    nc.vector.tensor_scalar(acc[:, i, :], acc[:, i, :], mv[:, i, 0:1], rstd[:, i:i + 1],
                                            ALU.subtract, ALU.mult).then_inc(s["h_done"], 1)

            @block.scalar
            def _(act):
                rsqrt_scalar(nc, act, s, var, lnv, r0)

            @block.gpsimd
            def _(pool):
                for i in range(TILES):
                    pool.wait_ge(s["h_done"], i + 1)
                    nc.gpsimd.tensor_tensor(acc[:, i, :], acc[:, i, :], x2[:, i, :], ALU.add).then_inc(s["y_added"], 1)

            @block.sync
            def _(sp):
                for i in range(4):
                    sp.wait_ge(s["y_added"], 8 * i + 8)
                    for b in range(2):
                        sp.dma_start(Ov[b][:, 8 * i:8 * i + 8, :],
                                     acc[C * b:C * b + C, 8 * i:8 * i + 8, :]).then_inc(s["stored"], 16)
                sp.wait_ge(s["stored"], 16 * 8)


def rsqrt_vector(nc, dve, s, mv, var, r0, nt, rstd, links):
    dve.wait_ge(s["link"], links)
    nc.vector.tensor_scalar(var[:], mv[:, :, 1], EPS, None, ALU.add).then_inc(s["var_ready"], 1)
    dve.wait_ge(s["guess_ready"], 1)
    dve.wait_ge(s["var_ready"], 1)
    nc.vector.tensor_tensor(nt[:], var[:], r0[:], ALU.mult).then_inc(s["link"], 1)
    dve.wait_ge(s["link"], links + 1)
    nc.vector.tensor_tensor(nt[:], nt[:], r0[:], ALU.mult).then_inc(s["link"], 1)
    dve.wait_ge(s["link"], links + 2)
    nc.vector.tensor_scalar(nt[:], nt[:], -0.5, 1.5, ALU.mult, ALU.add).then_inc(s["link"], 1)
    dve.wait_ge(s["link"], links + 3)
    nc.vector.tensor_tensor(rstd[:], nt[:], r0[:], ALU.mult).then_inc(s["rows_ready"], 1)


def rsqrt_scalar(nc, act, s, var, lnv, r0):
    act.wait_ge(s["var_ready"], 1)
    nc.scalar.activation(lnv[:], var[:], ACT.Ln).then_inc(s["a_link"], 1)
    act.wait_ge(s["a_link"], 1)
    nc.scalar.activation(r0[:], lnv[:], ACT.Exp, scale=-0.5).then_inc(s["guess_ready"], 1)


def load_expert(sp, a, wg, wu, wd, e, slot, sem):
    for w, src in ((wg, a["wg"]), (wu, a["wu"])):
        v = src.rearrange("e (k p) i -> e p k i", p=P)
        v = v[e] if isinstance(e, int) else v[bass.ds(e, 1)].rearrange("o p k i -> (o p) k i")
        sp.dma_start(w[:, slot, :, :], v).then_inc(sem, 16)
    v = a["wd"][e] if isinstance(e, int) else a["wd"][bass.ds(e, 1)].rearrange("o p d -> (o p) d")
    sp.dma_start(wd[:, slot, :], v).then_inc(sem, 16)


def route_block(nc, s, i, x2, xfT, coef, ident, rw, e_bias, mv, rstd, xf, xfs, score, sfc, work, top, gsum, gtop, grep,
                gmask, wsum, winv, ps):
    with nc.Block() as block:
        @block.vector
        def _(dve):
            links = [0]

            def link(ins):
                links[0] += 1
                ins.then_inc(s["link"], 1)
                dve.wait_ge(s["link"], links[0])

            link(nc.vector.tensor_copy(xf[:], x2[:, bass.ds(i * 4, 4), :]))
            link(nc.vector.tensor_copy(wsum[:], mv[:, bass.ds(i * 4, 4), 0]))
            link(nc.vector.tensor_copy(winv[:], rstd[:, bass.ds(i * 4, 4)]))
            for m in range(4):
                nc.vector.tensor_scalar(xf[:, m, :], xf[:, m, :], wsum[:, m:m + 1], winv[:, m:m + 1],
                                        ALU.subtract, ALU.mult).then_inc(s["xf_ready"], 1)
            dve.wait_ge(s["exp_ready"], 1)
            link(nc.vector.tensor_scalar(score[:], score[:], 1.0, None, ALU.add))
            link(nc.vector.reciprocal(score[:], score[:]))
            link(nc.vector.tensor_tensor(sfc[:], score[:], over(e_bias[:], 4), ALU.add))
            for m in range(4):
                for g in range(G):
                    last = nc.vector.max(top[:, m, g, :], sfc[:, m, 8 * g:8 * g + 8])
            link(last)
            link(nc.vector.tensor_tensor(gsum[:], top[:, :, :, 0], top[:, :, :, 1], ALU.add))
            for m in range(4):
                last = nc.vector.max(gtop[:, m, :], gsum[:, m, :])
            link(last)
            link(nc.vector.memset(gtop[:, :, 4:8], BIG))
            for m in range(4):
                last = nc.vector.match_replace(out=grep[:, m, :], in_to_replace=gtop[:, m, :], in_values=gsum[:, m, :],
                                               imm_value=-BIG)
            link(last)
            link(nc.vector.tensor_scalar(gmask[:], grep[:], -BIG, None, ALU.is_equal))
            link(nc.vector.tensor_tensor(sfc[:].rearrange("p m (g e) -> p (m g) e", e=8),
                                         sfc[:].rearrange("p m (g e) -> p (m g) e", e=8),
                                         bc(gmask[:].rearrange("p m g -> p (m g)"), 8), ALU.mult))
            for m in range(4):
                last = nc.vector.max(gtop[:, m, :], sfc[:, m, :])
            link(last)
            for m in range(4):
                last = nc.vector.match_replace(out=work[:, m, :], in_to_replace=gtop[:, m, :], in_values=sfc[:, m, :],
                                               imm_value=-BIG)
            link(last)
            link(nc.vector.tensor_scalar(work[:], work[:], -BIG, None, ALU.is_equal))
            link(nc.vector.tensor_tensor(work[:], work[:], score[:], ALU.mult))
            link(nc.vector.tensor_reduce(wsum[:], work[:], AX_X, ALU.add))
            link(nc.vector.tensor_scalar(wsum[:], wsum[:], 1e-20, None, ALU.add))
            link(nc.vector.reciprocal(winv[:], wsum[:]))
            link(nc.vector.tensor_scalar(winv[:], winv[:], SCALE, None, ALU.mult))
            nc.vector.tensor_tensor(coef[:, bass.ds(i * 4, 4), 0:E], work[:], bc(winv[:], E),
                                    ALU.mult).then_inc(s["coef_ready"], 1)

        @block.tensor
        def _(pe):
            for m in range(4):
                pe.wait_ge(s["xf_ready"], m + 1)
                for kt in range(2):
                    mm = nc.tensor.transpose(ps[kt][:, P * m:P * m + P], xf[:, m, P * kt:P * kt + P], ident[:])
            mm.then_inc(s["xfT_done"], 1)
            pe.wait_ge(s["xfT_copied"], 2)
            for m in range(4):
                for kt in range(2):
                    mm = nc.tensor.matmul(ps[2][:, E * m:E * m + E], xfs[:, kt, P * m:P * m + P], rw[:, kt, :],
                                          start=(kt == 0), stop=(kt == 1))
            mm.then_inc(s["logits_done"], 1)

        @block.scalar
        def _(act):
            act.wait_ge(s["xfT_done"], 1)
            for kt in range(2):
                nc.scalar.copy(xfs[:, kt, :], ps[kt][:, :]).then_inc(s["xfT_copied"], 1)
            act.wait_ge(s["logits_done"], 1)
            nc.scalar.activation(score[:], ps[2][:, 0:4 * E].rearrange("p (m e) -> p m e", e=E), ACT.Exp,
                                 scale=-1.0).then_inc(s["exp_ready"], 1)

        @block.gpsimd
        def _(pool):
            pool.wait_ge(s["xfT_copied"], 2)
            nc.gpsimd.tensor_copy(xfT[:, :, bass.ds(i * 512, 512)], xfs[:]).then_inc(s["xfT_kept"], 1)


def expert_pair(nc, s, a, i, more, wg, wu, wd, coef, coef_e, xfT, sg, h, acc, ps):
    STEPS = 2 * BLOCKS
    with nc.Block() as block:
        @block.sync
        def _(sp):
            load_expert(sp, a, wg, wu, wd, i * 2 + 1, 1, s["weights_loaded"])
            if more:
                sp.wait_ge(s["y_done"], 2 * BLOCKS)
                load_expert(sp, a, wg, wu, wd, i * 2 + 2, 0, s["next_loaded"])
                sp.wait_ge(s["next_loaded"], 48)
            sp.wait_ge(s["weights_loaded"], 48)

        @block.gpsimd
        def _(pool):
            src = coef[:, :, E:E + 2] if isinstance(i, int) else coef[:, :, bass.ds(i * 2, 2)]
            nc.gpsimd.tensor_copy(coef_e[:].rearrange("p e n -> p n e"), src).then_inc(s["coef_ready"], 1)

        @block.tensor
        def _(pe):
            def up(k):
                w = k // BLOCKS
                cols = slice(512 * (k % BLOCKS), 512 * (k % BLOCKS) + 512)
                if k == BLOCKS:
                    pe.wait_ge(s["weights_loaded"], 48)
                if k >= 2:
                    pe.wait_ge(s["h_done"], k - 1)
                for wt, b in ((wg, 0), (wu, 1)):
                    for kt in range(2):
                        mm = nc.tensor.matmul(ps[2 * (k % 2) + b][:, :], wt[:, w, kt, :], xfT[:, kt, cols],
                                              start=(kt == 0), stop=(kt == 1))
                mm.then_inc(s["gu_done"], 1)

            def down(k):
                pe.wait_ge(s["h_done"], k + 1)
                for m in range(4):
                    if m % 2 == 0 and 2 * k + m // 2 >= 4:
                        pe.wait_ge(s["y_added"], 4 * (k - 2) + 2 * (m // 2) + 2)
                    mm = nc.tensor.matmul(ps[4 + 2 * (k % 2) + m // 2][:, 256 * (m % 2):256 * (m % 2) + 256],
                                          h[:, k % 2, P * m:P * m + P], wd[:, k // BLOCKS, :], start=True, stop=True)
                    if m % 2 == 1:
                        mm.then_inc(s["y_done"], 1)

            for k in range(STEPS + 1):
                if k < STEPS:
                    up(k)
                if k >= 1:
                    down(k - 1)

        @block.scalar
        def _(act):
            for k in range(STEPS):
                act.wait_ge(s["gu_done"], k + 1)
                if k >= 2:
                    act.wait_ge(s["h_done"], k - 1)
                nc.scalar.activation(sg[:, k % 2, :], ps[2 * (k % 2)][:, :], ACT.Silu).then_inc(s["silu_done"], 1)

        @block.vector
        def _(dve):
            dve.wait_ge(s["coef_ready"], 1)

            def gate(k):
                dve.wait_ge(s["silu_done"], k + 1)
                if k >= 2:
                    dve.wait_ge(s["y_done"], 2 * (k - 1))
                nc.vector.tensor_tensor(h[:, k % 2, :], ps[2 * (k % 2) + 1][:, :], sg[:, k % 2, :],
                                        ALU.mult).then_inc(s["h_done"], 1)

            def add(k):
                for m in range(4):
                    if m % 2 == 0:
                        dve.wait_ge(s["y_done"], 2 * k + m // 2 + 1)
                    tile = 4 * (k % BLOCKS) + m
                    if k >= BLOCKS:
                        dve.wait_ge(s["y_added"], 4 * (k - BLOCKS) + m + 1)
                    nc.vector.scalar_tensor_tensor(
                        out=acc[:, tile, :], in0=ps[4 + 2 * (k % 2) + m // 2][:, 256 * (m % 2):256 * (m % 2) + 256],
                        scalar=coef_e[:, k // BLOCKS, tile:tile + 1], in1=acc[:, tile, :],
                        op0=ALU.mult, op1=ALU.add).then_inc(s["y_added"], 1)

            for k in range(STEPS + 1):
                if k < STEPS:
                    gate(k)
                if k >= 1:
                    add(k - 1)


def program(nc, a, out):
    scratch = nc.dram_tensor("x2_scratch", (TILES + 1, P, 256), F32, kind="Internal").ap()
    attention_stage(nc, a, scratch)
    moe_stage(nc, a, scratch, out)


def layouts(np, d):
    def f(name):
        return np.asarray(d[name])

    def kt(w):
        return w.T.reshape(2, P, -1).transpose(1, 0, 2)

    a = {}
    a["x"] = f("L0_attn_x")
    a["wq"], a["wk"], a["wa"], a["war"] = (kt(f("L0_attn_" + n)) for n in ("Wq", "Wk", "Wa", "WaR"))
    wv = kt(f("L0_attn_Wv")).reshape(P, 2, 8, 2, C)
    a["wv"] = wv.transpose(0, 1, 3, 2, 4).reshape(P, 2, 2, 512)
    a["wo"] = f("L0_attn_Wo").T.reshape(8, P, 256).transpose(1, 0, 2)
    bg = np.stack([f("L0_attn_Wb"), f("L0_attn_Wg")])
    bg = bg.reshape(2, 8, 2, 2, P)
    a["wbg"] = bg.transpose(4, 3, 2, 0, 1).reshape(P, 2, 2, 16)
    gb = np.stack([f("L0_attn_ba"), f("L0_attn_baR")]).reshape(2, 8, P)
    a["gate_bias"] = gb.transpose(2, 0, 1)
    b2 = np.stack([f("L0_attn_bb"), f("L0_attn_bg")]).reshape(2, 8, 2).transpose(2, 0, 1)
    a["bg_bias"] = np.broadcast_to(b2[:, None, :, :, None], (2, C, 2, 8, 2)).reshape(P, 2, 16)
    a["lnw"], a["lnb"] = f("L0_attn_ln_w").reshape(2, P).T, f("L0_attn_ln_b").reshape(2, P).T
    a["rw"] = f("L0_ffn_router_w").T.reshape(2, P, E).transpose(1, 0, 2)
    a["e_bias"] = np.broadcast_to(f("L0_ffn_e_bias")[None, :], (P, E))
    for n, s in (("wg", "SWg"), ("wu", "SWu")):
        shared = f("L0_ffn_" + s).reshape(256, 2, P).transpose(1, 0, 2)
        a[n] = np.concatenate([f("L0_ffn_W" + n[1]), shared])
    a["wd"] = np.concatenate([f("L0_ffn_Wd"), f("L0_ffn_SWd").reshape(2, P, 256)])

    r, c = np.arange(C)[:, None], np.arange(C)[None, :]
    two = lambda m: np.concatenate([m, m]).astype(np.float32)
    a["ident"] = np.eye(P, dtype=np.float32)
    a["eye"] = two(r == c)
    a["strict"] = two(r > c)
    a["pair_mask"] = two((r // 2 == c // 2) & (r >= c))[:, 0:Q] + two((r // 2 == c // 2) & (r >= c))[:, Q:C]
    m = [(r == c) | ((r // (2 * b) == c // (2 * b)) & (r // b % 2 == 0) & (c // b % 2 == 1)) for b in (2, 4, 8, 16)]
    a["merge_mask"] = np.stack([two(x)[:, 0:Q] + two(x)[:, Q:C] for x in m], axis=1)
    a["pq_mask"] = np.stack([two(r < c), two(r <= c)], axis=1)
    a["restart"] = np.broadcast_to((np.arange(1024) % C != 0).astype(np.float32)[None, :], (P, 1024))
    return {k: np.ascontiguousarray(v) for k, v in a.items()}


def kernel(**inputs):
    import numpy as _np
    import concourse.bacc as _bacc
    from concourse import mybir as _mybir
    from concourse.bass_utils import run_bass_kernel_spmd as _run

    nc = _bacc.Bacc("TRN2", target_bir_lowering=False, num_devices=1)
    arrays, aps = {}, {}
    for name, arr in layouts(_np, inputs).items():
        arrays[f"in_{name}_dram"] = arr
        aps[name] = nc.dram_tensor(f"in_{name}_dram", arr.shape, _mybir.dt.from_np(arr.dtype), kind="ExternalInput").ap()
    out = nc.dram_tensor("out_0_dram", (2, 2048, 256), _mybir.dt.float32, kind="ExternalOutput").ap()
    program(nc, aps, out)
    r = _run(nc, [arrays], core_ids=[0])
    return r.results[0]["out_0_dram"]
```

```python
from contextlib import ExitStack

import concourse.bass as bass
from concourse import mybir

ALU = mybir.AluOpType
ACT = mybir.ActivationFunctionType
F32 = mybir.dt.float32
AX_X = mybir.AxisListType.X

P = 128
C = 64
NB = 3
Q = 32
LEVELS = 4
EPS = 1e-5
K_TINY = 1e-24
STREAMS = [(0, 0), (1, 0), (0, 1), (1, 1)]

E = 64
G = 8
SCALE = 2.5
BIG = 3.0e38
RUN = 33
GROUPS = [range(0, 16), range(16, 32), range(32, 49), range(49, 66)]

SMALL = {"V": "act", "KT": "act", "A": "dve", "PQ": "dve", "RQ": "dve", "Y": "dve", "N": "act", "Z": "act", "X": "act",
         "KS": "dve", "KR": "dve", "U": "act", "PR": "dve", "W": "act", "O": "act", "SU": "dve", "RU": "dve",
         "OUT": "dve"}
SHARE = {"V": 0.93, "KT": 1.24, "A": 0.76, "PQ": 0.5, "RQ": 1.15, "Y": 3.36, "N": 4.0, "Z": 2.0, "X": 2.41, "KS": 0.97,
         "KR": 1.01, "U": 1.55, "PR": 1.34, "W": 3.03, "O": 2.47, "mid_O": 2.84, "SU": 1.63, "RU": 1.49, "OUT": 1.12}
WIDE = {"SB": "dve", "RT": "act", "RL": "act", "XT": "act", "a": "dve", "r": "dve", "k": "act", "q": "act"}


def order_of_jobs(chunk, front):
    if not chunk:
        return [("RT", ""), ("RL", "")]
    jobs = [("SB", ""), ("V", "0"), ("V", "1")] + [("KT", f"{g}{h}") for g in range(2) for h in range(2)]
    jobs += [("A", f"{g}{h}") for g, h in STREAMS] + [("RT", "")] + [("PQ", str(i)) for i in range(4)]
    jobs += [("RL", ""), ("RQ", "0"), ("RQ", "1")] + [("XT", "")] * front
    for l in range(1, LEVELS + 1):
        for g in range(2):
            jobs += [("Y", f"{l}{g}")] + [("arkq"[l - 1], str(g))] * front
        jobs += [("N", f"{l}{g}") for g in range(2)]
    for kind in ("Z", "X", "KS", "KR", "U", "PR", "W", "O", "SU", "RU"):
        for h in "01":
            jobs += [(kind, h)] + [("mid_O", h)] * (kind == "O")
    return jobs + [("OUT", "")]


class Order:

    def __init__(self, chunk, front, experts):
        jobs = order_of_jobs(chunk, front)
        self.experts = experts
        steps, total, share, last = 3 * len(experts), sum(SHARE.get(kind, 0) for kind, _ in jobs), 0, len(jobs) - 1
        places = []
        for n, (kind, _) in enumerate(jobs):
            share += SHARE.get(kind, 0)
            while len(places) < steps and (len(places) + 0.5) / steps <= share / total:
                places.append(max(n, places[-1] + 1) if len(places) % 3 == 2 else max([n] + places[-1:]))
        self.last = last
        self.gate, self.up, self.down = places[0::3], places[1::3], places[2::3]
        assert all(u < d <= last for u, d in zip(self.up, self.down))
        self.place = {kind + i: n for n, (kind, i) in enumerate(jobs)}
        self.engine, self.emptied, self.done, self.before = {}, {}, {}, {}
        for table, banks in ((SMALL, NB), (WIDE, 1)):
            mine = [(kind, kind + i) for kind, i in jobs if kind in table]
            for n, (kind, name) in enumerate(mine):
                self.engine[name] = table[kind]
                self.done[name] = n + 1
                self.before[name] = mine[n - banks][1] if n >= banks else None
                self.emptied[name] = sum(table[k] == table[kind] for k, _ in mine[:n + 1])


class Tensors:
    pass


def semaphores(nc, ctx, names):
    sems = {n: ctx.enter_context(nc.semaphore(n)) for n in names}
    return sems, [sems[n] for n in names]


def alloc_attention(nc, ctx):
    t = Tensors()

    def sb(name, shape):
        return ctx.enter_context(nc.sbuf_tensor(name, shape, F32))

    t.wq, t.wk, t.wa, t.war = (sb(n, [P, 2, 1024]) for n in ("wq", "wk", "wa", "war"))
    t.wv = sb("wv", [P, 2, 2, 512])
    t.wo = sb("wo", [P, 8, 256])
    t.wbg = sb("wbg", [P, 2, 2, 16])
    t.gate_bias = sb("gate_bias", [P, 2, 8])
    t.bg_bias = sb("bg_bias", [P, 2, 16])
    t.lnw, t.lnb = sb("lnw", [P, 2]), sb("lnb", [P, 2])
    t.ident = sb("ident", [P, P])
    t.eye = sb("eye", [P, C])
    t.strict = sb("strict", [P, C])
    t.pair_mask = sb("pair_mask", [P, Q])
    t.merge_mask = sb("merge_mask", [P, LEVELS, Q])
    t.pq_mask = sb("pq_mask", [P, 2, C])
    t.restart = ctx.enter_context(nc.sbuf_tensor("restart", [P, 1024], mybir.dt.bfloat16))
    t.ones = sb("ones", [P, 1])

    t.S, t.R = sb("S", [P, 16, C]), sb("R", [P, 16, C])
    t.x_new, t.x_res = sb("x_new", [P, 256]), sb("x_res", [P, 256])
    t.res, t.res_new = sb("res", [P, 256]), sb("res_new", [P, 256])
    t.xhat, t.y = sb("xhat", [P, 256]), sb("y", [P, 256])
    t.stats, t.mv, t.ln_tmp = sb("stats", [P, 4, 6]), sb("mv", [P, 4, 2]), sb("ln_tmp", [P, 4, 8])
    t.xnT = sb("xnT", [P, 2, P])
    t.z = sb("z", [P, 2, 1024])
    t.c = sb("c", [P, 2, 16, C])
    t.dec = t.z[:].rearrange("p g (u n) -> p g u n", n=C)
    t.dec_end = sb("dec_end", [P, 2, 16])
    t.k, t.q = sb("k", [P, 16, C]), sb("q", [P, 16, C])
    t.kplus = [sb("kplus_s", [P, 16, C]), sb("kplus_r", [P, 16, C])]
    t.kminus = [t.c[:, 0, :, :], t.c[:, 1, :, :]]
    t.pq = sb("pq", [P, 2, 16, C])
    t.rqplus = sb("rqplus", [P, 16, C])
    t.V, t.bv = sb("V", [P, 16, C]), sb("bv", [P, 16, C])
    t.sc = sb("sc", [P, 8, 16])
    t.bgz = sb("bgz", [P, 2, 16])
    t.bg = sb("bg", [P, 2, 16])
    t.bn, t.nbn2 = sb("bn", [P, 2, 16]), sb("nbn2", [P, 2, 16])
    t.L = [sb("L_s", [P, 16, C]), sb("L_r", [P, 16, C])]
    t.T = [sb("T_s", [P, 16, Q]), sb("T_r", [P, 16, Q])]
    t.N = [sb("N_s", [P, 16, Q]), sb("N_r", [P, 16, Q])]
    t.Y = [sb("Y_s", [P, 16, Q]), sb("Y_r", [P, 16, Q])]
    t.inv = [sb("inv_s", [P, 16, C]), sb("inv_r", [P, 16, C])]
    t.pqT = sb("pqT", [P, 16, 2, C])
    t.rqT = sb("rqT", [P, 16, C])
    t.kT = [sb("kT_s", [P, 16, C]), sb("kT_r", [P, 16, C])]
    t.B, t.U = t.L
    t.BR = sb("BR", [P, 16, C])

    t.rw, t.e_bias = sb("rw", [P, 2, E]), sb("e_bias", [P, E])
    t.xf, t.xfs = sb("xf", [P, 256]), sb("xfs", [P, 2, P])
    t.xfT_new, t.xfT = sb("xfT_new", [P, 2, 5, P]), sb("xfT", [P, 2, 4, P])
    t.coef_new, t.coef = sb("coef_new", [P, 5, E]), sb("coef", [P, 4, E + 2])
    t.acc, t.rows = sb("acc", [P, 4, 256]), sb("rows", [P, 4, 256])
    t.wg, t.wu, t.wd = sb("wg", [P, 2, 2, P]), sb("wu", [P, 2, 2, P]), sb("wd", [P, 2, 256])
    t.coef_run = sb("coef_run", [P, 4, RUN])
    t.h = sb("h", [P, 512])
    t.score, t.sfc, t.work = sb("score", [P, E]), sb("sfc", [P, E]), sb("work", [P, E])
    t.top = sb("top", [P, G, 8])
    t.gsum, t.gtop, t.grep, t.gmask = (sb(n, [P, 8]) for n in ("gsum", "gtop", "group_rep", "gmask"))
    t.wsum = sb("wsum", [P, 2])
    t.fin_stats, t.fin_mv, t.fin_tmp = sb("fin_stats", [P, 4, 6]), sb("fin_mv", [P, 4, 2]), sb("fin_tmp", [P, 6, 4])
    t.ps = [ctx.enter_context(nc.psum_tensor(f"bank{i}", [P, 512], F32)) for i in range(8)]

    names = ["consts_loaded", "x_loaded", "x_res_loaded",
             "mm_done", "front_mm", "dve_emptied", "act_emptied", "front_dve", "front_act",
             "dve_link", "act_link", "ln_var_ready", "ln_guess_ready", "xhat_ready", "x2_made", "dec_end_ready",
             "res_copied", "norm_sq_ready", "norm_guess_ready", "bg_exp_ready",
             "scales_ready", "coef_ready", "L_ready", "T0_ready", "restart_ready", "N0_ready",
             "T_ready", "inv_ready", "bv_ready", "B_ready", "BR0_ready", "BR1_ready",
             "scan_done", "log_ready", "dec_ready", "plus_made", "states_ready", "pool_link", "xf_ready", 
             "x2_stored", "x2_loaded", "xfT_kept", "block_ready", "g_done", "u_done", "sig_ready", "h_ready",
             "y_done", "y_added", "weights_loaded", "next_loaded", "fin_var", "fin_guess", "fin_rows", "fin_added",
             "out_stored"]
    t.sem, t.sems = semaphores(nc, ctx, names)
    return t


def wait_emptied(eng, t, o, name):
    wide = name.rstrip("01234") in WIDE
    eng.wait_ge(t.sem["front_" + o.engine[name] if wide else o.engine[name] + "_emptied"], o.emptied[name])


def slot_of(ap, dim, slot):
    if isinstance(slot, int):
        return ap[:, slot] if dim == 1 else ap[:, :, slot]
    if dim == 1:
        return ap[:, bass.ds(slot, 1), :].rearrange("p o n -> p (o n)")
    return ap[:, :, bass.ds(slot, 1), :].rearrange("p k o n -> p k (o n)")


def bc(ap, n):
    p, u = ap.shape
    return ap.rearrange("p (u o) -> p u o", o=1).broadcast_to([p, u, n])


def over(ap, u):
    p, n = ap.shape
    return ap.rearrange("p (o n) -> p o n", o=1).broadcast_to([p, u, n])


def blk(ap):
    return ap.rearrange("p (u n) -> p u n", n=C)


def weight_slot(t, e):
    return t.wg[:, e % 2, :, :], t.wu[:, e % 2, :, :], t.wd[:, e % 2, :]


def load_expert(sp, a, wg, wu, wd, e, sem):
    for w, src in ((wg, a["wg"]), (wu, a["wu"])):
        v = src.rearrange("e (k p) i -> e p k i", p=P)
        v = v[e] if isinstance(e, int) else v[bass.ds(e, 1)].rearrange("o p k i -> (o p) k i")
        sp.dma_start(w, v).then_inc(sem, 16)
    v = a["wd"][e] if isinstance(e, int) else a["wd"][bass.ds(e, 1)].rearrange("o p d -> (o p) d")
    sp.dma_start(wd, v).then_inc(sem, 16)



class ExpertsOnTensor:
    def __init__(self, nc, pe, t, o, first):
        self.nc, self.pe, self.t, self.o, self.first = nc, pe, t, o, first
        self.place = 0

    def through(self, place):
        while self.place <= place:
            for i in range(len(self.o.experts)):
                if self.place == self.o.gate[i]:
                    self.gate(i)
                if self.place == self.o.up[i]:
                    self.up(i)
                if self.place == self.o.down[i]:
                    self.down(i)
            self.place += 1

    def gate(self, i):
        if i == 0 and self.first:
            self.pe.wait_ge(self.t.sem["block_ready"], 1)
        if i >= 1:
            self.pe.wait_ge(self.t.sem["weights_loaded"], 48 * i)
            self.pe.wait_ge(self.t.sem["h_ready"], i)
        self.product(self.t.ps[NB + 1], self.t.wg, i).then_inc(self.t.sem["g_done"], 1)

    def up(self, i):
        self.product(self.t.ps[NB + 2], self.t.wu, i).then_inc(self.t.sem["u_done"], 1)

    def product(self, ps, w, i):
        for kt in range(2):
            mm = self.nc.tensor.matmul(ps[:, :], w[:, self.o.experts[i] % 2, kt, :],
                                       self.t.xfT[:, kt, :, :].rearrange("p m n -> p (m n)"),
                                       start=(kt == 0), stop=(kt == 1))
        return mm

    def down(self, i):
        self.pe.wait_ge(self.t.sem["h_ready"], i + 1)
        for m in range(4):
            if m % 2 == 0 and i >= 1:
                self.pe.wait_ge(self.t.sem["y_added"], 2 * (i - 1) + m // 2 + 1)
            mm = self.nc.tensor.matmul(self.t.ps[NB + 3 + m // 2][:, 256 * (m % 2):256 * (m % 2) + 256],
                                       self.t.h[:, P * m:P * m + P], self.t.wd[:, self.o.experts[i] % 2, :],
                                       start=True, stop=True)
            if m % 2 == 1:
                mm.then_inc(self.t.sem["y_done"], 1)


class ExpertsOnScalar:
    def __init__(self, nc, act, t, o, link):
        self.nc, self.act, self.t, self.o, self.link = nc, act, t, o, link
        self.place = 0

    def through(self, place):
        while self.place <= place:
            for i in range(len(self.o.experts)):
                if self.place == self.o.gate[i]:
                    self.sigmoid(i)
            self.place += 1

    def sigmoid(self, i):
        self.act.wait_ge(self.t.sem["g_done"], i + 1)
        self.link(self.nc.scalar.activation(self.t.h[:], self.t.ps[NB + 1][:, :], ACT.Exp, scale=-1.0))
        self.link(self.nc.scalar.activation(self.t.h[:], self.t.h[:], ACT.Ln, bias=1.0))
        self.nc.scalar.activation(self.t.h[:], self.t.h[:], ACT.Exp, scale=-1.0).then_inc(self.t.sem["sig_ready"], 1)


class ExpertsOnVector:
    def __init__(self, nc, dve, t, o, link, finish):
        self.nc, self.dve, self.t, self.o, self.link, self.finish = nc, dve, t, o, link, finish
        self.place = 0

    def through(self, place):
        while self.place <= place:
            for i in range(len(self.o.experts)):
                if self.place == self.o.up[i]:
                    self.hidden(i)
            for i in range(len(self.o.experts)):
                if self.place == self.o.down[i]:
                    self.add(i)
            self.place += 1

    def hidden(self, i):
        self.dve.wait_ge(self.t.sem["sig_ready"], i + 1)
        self.link(self.nc.vector.tensor_tensor(self.t.h[:], self.t.ps[NB + 1][:, :], self.t.h[:], ALU.mult))
        self.dve.wait_ge(self.t.sem["u_done"], i + 1)
        self.nc.vector.tensor_tensor(self.t.h[:], self.t.ps[NB + 2][:, :], self.t.h[:], ALU.mult).then_inc(
            self.t.sem["h_ready"], 1)

    def add(self, i):
        e = self.o.experts[i]
        if i == 0 and self.finish:
            self.dve.wait_ge(self.t.sem["fin_added"], 4)
        for m in range(4):
            if m % 2 == 0:
                self.dve.wait_ge(self.t.sem["y_done"], 2 * i + m // 2 + 1)
                if i >= 1:
                    self.dve.wait_ge(self.t.sem["y_added"], 2 * (i - 1) + m // 2 + 1)
            y, acc = self.t.ps[NB + 3 + m // 2][:, 256 * (m % 2):256 * (m % 2) + 256], self.t.acc[:, m, :]
            if e == 0:
                ins = self.nc.vector.tensor_scalar(acc, y, self.t.coef[:, m, e:e + 1], None, ALU.mult)
            else:
                ins = self.nc.vector.scalar_tensor_tensor(out=acc, in0=y, scalar=self.t.coef[:, m, e:e + 1], in1=acc,
                                                          op0=ALU.mult, op1=ALU.add)
            if m % 2 == 1:
                ins.then_inc(self.t.sem["y_added"], 1)


def block_in_place(nc, pool, t):
    nc.gpsimd.tensor_copy(t.xfT[:], t.xfT_new[:, :, 1:5, :])
    nc.gpsimd.tensor_copy(t.coef[:, :, 0:E], t.coef_new[:, 1:5, :]).then_inc(t.sem["block_ready"], 1)
    pool.wait_ge(t.sem["block_ready"], 1)


def route_scores(nc, t, link):
    link(nc.vector.tensor_scalar(t.score[:], t.score[:], 1.0, None, ALU.add))
    link(nc.vector.reciprocal(t.score[:], t.score[:]))
    link(nc.vector.tensor_tensor(t.sfc[:], t.score[:], t.e_bias[:], ALU.add))
    for g in range(G):
        last = nc.vector.max(t.top[:, g, :], t.sfc[:, 8 * g:8 * g + 8])
    link(last)
    link(nc.vector.tensor_tensor(t.gsum[:], t.top[:, :, 0], t.top[:, :, 1], ALU.add))


def route_groups(nc, t, link):
    link(nc.vector.max(t.gtop[:], t.gsum[:]))
    link(nc.vector.memset(t.gtop[:, 4:8], BIG))
    link(nc.vector.match_replace(out=t.grep[:], in_to_replace=t.gtop[:], in_values=t.gsum[:], imm_value=-BIG))
    link(nc.vector.tensor_scalar(t.gmask[:], t.grep[:], -BIG, None, ALU.is_equal))
    link(nc.vector.tensor_tensor(t.sfc[:].rearrange("p (g e) -> p g e", e=8),
                                 t.sfc[:].rearrange("p (g e) -> p g e", e=8), bc(t.gmask[:], 8), ALU.mult))


def route_best(nc, t, link, slot):
    link(nc.vector.max(t.gtop[:], t.sfc[:]))
    link(nc.vector.match_replace(out=t.work[:], in_to_replace=t.gtop[:], in_values=t.sfc[:], imm_value=-BIG))
    link(nc.vector.tensor_scalar(t.work[:], t.work[:], -BIG, None, ALU.is_equal))
    link(nc.vector.tensor_tensor(t.work[:], t.work[:], t.score[:], ALU.mult))
    link(nc.vector.tensor_reduce(t.wsum[:, 0:1], t.work[:], AX_X, ALU.add))
    link(nc.vector.tensor_scalar(t.wsum[:, 0:1], t.wsum[:, 0:1], 1e-20, None, ALU.add))
    link(nc.vector.reciprocal(t.wsum[:, 1:2], t.wsum[:, 0:1]))
    link(nc.vector.tensor_scalar(slot_of(t.coef_new, 1, slot), t.work[:], t.wsum[:, 1:2], SCALE, ALU.mult, ALU.mult))


def body(nc, t, a, n, X, scratch, slot, front, experts=(), first=False, prefetch=None, finish=None):
    o = Order(True, front, experts)
    with nc.Block() as block:
        half = [slice(8 * h, 8 * h + 8) for h in range(2)]

        def bank(name):
            return t.ps[NB if name.rstrip("01234") in WIDE else (o.done[name] - 1) % NB]

        @block.sync
        def _(sp):
            if experts:
                load_expert(sp, a, *weight_slot(t, experts[1]), experts[1], t.sem["weights_loaded"])
            if front:
                for b in range(2):
                    sp.dma_start(t.x_new[C * b:C * b + C, :], X(n + 1, b)).then_inc(t.sem["x_loaded"], 16)
            sp.wait_ge(t.sem["x2_made"], 1)
            sp.dma_start(scratch(n), t.y[:, :]).then_inc(t.sem["x2_stored"], 16)
            for b in range(2):
                sp.dma_start(t.x_res[C * b:C * b + C, :], X(n, b)).then_inc(t.sem["x_res_loaded"], 16)
            if front:
                sp.wait_ge(t.sem["x_loaded"], 32)
            sp.wait_ge(t.sem["x_res_loaded"], 32)
            sp.wait_ge(t.sem["x2_stored"], 16)
            if finish:
                out, x2_rows, b = finish
                finish_load(sp, t, x2_rows, b)
                finish_store(sp, t, out, b)
            for i in range(2, len(experts)):
                sp.wait_ge(t.sem["y_done"], 2 * (i - 1))
                sp.wait_ge(t.sem["weights_loaded"], 48 * (i - 1))
                load_expert(sp, a, *weight_slot(t, experts[i]), experts[i], t.sem["weights_loaded"])
            if experts:
                sp.wait_ge(t.sem["weights_loaded"], 48 * (len(experts) - 1))
            if finish:
                sp.wait_ge(t.sem["out_stored"], 32)
            if prefetch is not None:
                sp.wait_ge(t.sem["y_done"], 2 * (len(experts) - 1))
                load_expert(sp, a, *weight_slot(t, prefetch), prefetch, t.sem["next_loaded"])
                sp.wait_ge(t.sem["next_loaded"], 48)

        @block.tensor
        def _(pe):
            moe = ExpertsOnTensor(nc, pe, t, o, first)

            def begin(name):
                moe.through(o.place[name])
                if o.before[name]:
                    wait_emptied(pe, t, o, o.before[name])
                return bank(name)

            def units(name, h, pairs, last=True):
                ps = begin(name)
                for i, u in enumerate(range(8 * h, 8 * h + 8)):
                    if i == 4 and "mid_" + name in o.place:
                        moe.through(o.place["mid_" + name])
                    for m, (lhsT, rhs) in enumerate(pairs):
                        for j in range(2):
                            r = slice(C * j, C * j + C)
                            mm = nc.tensor.matmul(ps[r, C * i:C * i + C], lhsT(r, u), rhs(r, u),
                                                  start=(m == 0), stop=(m == len(pairs) - 1))
                mm.then_inc(t.sem["mm_done"], 1)

            def of(x):
                return lambda r, u: x[r, u, :]

            def projection(name, w, i):
                ps = begin(name)
                for m in range(4):
                    for kt in range(2):
                        hp = 4 * i + m
                        mm = nc.tensor.matmul(ps[:, P * m:P * m + P], w[:, kt, P * hp:P * hp + P],
                                              t.xnT[:, kt, :], start=(kt == 0), stop=(kt == 1))
                mm.then_inc(t.sem["front_mm"], 1)

            ps = begin("SB")
            for u in range(16):
                for j in range(2):
                    r = slice(C * j, C * j + C)
                    nc.tensor.matmul(ps[r, u:u + 1], t.BR[r, u, :], t.ones[r, :], start=True, stop=True)
            for b in range(2):
                for kt in range(2):
                    for j in range(2):
                        r = slice(C * j, C * j + C)
                        mm = nc.tensor.matmul(ps[r, 16 + b:48 + b:2], t.xnT[:, kt, C * b:C * b + C],
                                              t.wbg[:, kt, j, :], start=(kt == 0), stop=(kt == 1))
            mm.then_inc(t.sem["front_mm"], 1)
            for h in range(2):
                ps = begin(f"V{h}")
                for b in range(2):
                    for kt in range(2):
                        for j in range(2):
                            r = slice(C * j, C * j + C)
                            dst = ps[r, :].rearrange("p (m b d) -> p m b d", b=2, d=C)[:, :, b, :]
                            mm = nc.tensor.matmul(dst, t.xnT[:, kt, C * b:C * b + C],
                                                  t.wv[:, kt, j, 256 * h:256 * h + 256],
                                                  start=(kt == 0), stop=(kt == 1))
                mm.then_inc(t.sem["mm_done"], 1)
            for g in range(2):
                for h in range(2):
                    units(f"KT{g}{h}", h, [(of(t.kminus[g]), lambda r, u: t.eye[r, :])])
            for g, h in STREAMS:
                units(f"A{g}{h}", h, [(of(t.kplus[g]), of(t.kminus[g]))])
            ps = begin("RT")
            pe.wait_ge(t.sem["xf_ready"], 1)
            for kt in range(2):
                mm = nc.tensor.transpose(ps[:, P * kt:P * kt + P], t.xf[:, P * kt:P * kt + P], t.ident[:, :])
            mm.then_inc(t.sem["front_mm"], 1)
            for i in range(4):
                ps = begin(f"PQ{i}")
                for m in range(4):
                    u = 4 * i + m
                    for j in range(2):
                        r = slice(C * j, C * j + C)
                        mm = nc.tensor.matmul(ps[r, 2 * C * m:2 * C * m + 2 * C], t.kminus[0][r, u, :],
                                              t.pq[r, :, u, :], start=True, stop=True)
                mm.then_inc(t.sem["mm_done"], 1)
            ps = begin("RL")
            for kt in range(2):
                mm = nc.tensor.matmul(ps[:, 0:E], t.xfs[:, kt, :], t.rw[:, kt, :], start=(kt == 0), stop=(kt == 1))
            mm.then_inc(t.sem["front_mm"], 1)
            for h in range(2):
                units(f"RQ{h}", h, [(of(t.kminus[1]), of(t.rqplus))])
            if front:
                ps = begin("XT")
                pe.wait_ge(t.sem["xhat_ready"], 1)
                for kt in range(2):
                    mm = nc.tensor.transpose(ps[:, P * kt:P * kt + P], t.xhat[:, P * kt:P * kt + P], t.ident[:, :])
                mm.then_inc(t.sem["front_mm"], 1)
            def blocks(name, lhsT, rhs):
                ps = begin(name)
                for u in range(16):
                    for q in range(4):
                        r = slice(Q * q, Q * q + Q)
                        mm = nc.tensor.matmul(ps[r, Q * u:Q * u + Q], lhsT(r, q, u), rhs[r, u, :], start=True, stop=True)
                mm.then_inc(t.sem["mm_done"], 1)

            for l in range(1, LEVELS + 1):
                if front:
                    if l == 1:
                        moe.through(o.place["Y10"])
                        wait_emptied(pe, t, o, "XT")
                    name, w = [("a", t.wa), ("r", t.war), ("k", t.wk), ("q", t.wq)][l - 1]
                for g in range(2):
                    moe.through(o.place[f"Y{l}{g}"])
                    if l == 1:
                        pe.wait_ge(t.sem["N0_ready"], g + 1)
                    else:
                        wait_emptied(pe, t, o, f"N{l - 1}{g}")
                    blocks(f"Y{l}{g}", lambda r, q, u: t.L[g][r, u, Q * (q % 2):Q * (q % 2) + Q], t.N[g])
                    if front:
                        projection(f"{name}{g}", w, g)
                for g in range(2):
                    moe.through(o.place[f"N{l}{g}"])
                    wait_emptied(pe, t, o, f"Y{l}{g}")
                    if l > 1:
                        pe.wait_ge(t.sem["T_ready"], 2 * (l - 2) + g + 1)
                    blocks(f"N{l}{g}", lambda r, q, u: t.T[g][r, u, :], t.Y[g])
            for g in range(2):
                moe.through(o.place[f"Z{g}"])
                wait_emptied(pe, t, o, f"N{LEVELS}{g}")
                ps = begin(f"Z{g}")
                for u in range(16):
                    for j in range(2):
                        top, low = slice(C * j, C * j + Q), slice(C * j + Q, C * j + C)
                        mm = nc.tensor.matmul(ps[top, Q * u:Q * u + Q], t.L[g][low, u, 0:Q], t.N[g][low, u, :],
                                              start=True, stop=True)
                mm.then_inc(t.sem["mm_done"], 1)
            for g in range(2):
                moe.through(o.place[f"X{g}"])
                wait_emptied(pe, t, o, f"Z{g}")
                pe.wait_ge(t.sem["T_ready"], 2 * (LEVELS - 1) + g + 1)
                ps = begin(f"X{g}")
                for u in range(16):
                    for j in range(2):
                        top = slice(C * j, C * j + Q)
                        mm = nc.tensor.matmul(ps[top, Q * u:Q * u + Q], t.T[g][top, u, :], t.Y[g][top, u, :],
                                              start=True, stop=True)
                mm.then_inc(t.sem["mm_done"], 1)
            for h in range(2):
                units(f"KS{h}", h, [(of(t.kplus[0]), of(t.S))])
            for h in range(2):
                units(f"KR{h}", h, [(of(t.kplus[1]), of(t.R))])
            for h in range(2):
                moe.through(o.place[f"U{h}"])
                pe.wait_ge(t.sem["B_ready"], h + 1)
                wait_emptied(pe, t, o, "X0")
                pe.wait_ge(t.sem["inv_ready"], 1)
                units(f"U{h}", h, [(of(t.inv[0]), of(t.B))])
            for h in range(2):
                moe.through(o.place[f"PR{h}"])
                wait_emptied(pe, t, o, f"U{h}")
                units(f"PR{h}", h, [(lambda r, u: t.pq[r, 0, u, :], of(t.S)),
                                    (lambda r, u: t.pqT[r, u, 0, :], of(t.U))])
            for h in range(2):
                moe.through(o.place[f"W{h}"])
                pe.wait_ge(t.sem["BR0_ready" if h == 0 else "BR1_ready"], 1)
                wait_emptied(pe, t, o, "X1")
                pe.wait_ge(t.sem["inv_ready"], 2)
                units(f"W{h}", h, [(of(t.inv[1]), of(t.BR))])
            for h in range(2):
                moe.through(o.place[f"O{h}"])
                wait_emptied(pe, t, o, f"W{h}")
                units(f"O{h}", h, [(of(t.S), lambda r, u: t.pq[r, 1, u, :]),
                                   (of(t.U), lambda r, u: t.pqT[r, u, 1, :]),
                                   (of(t.R), of(t.rqplus)),
                                   (of(t.B), of(t.rqT))])
            for h in range(2):
                units(f"SU{h}", h, [(of(t.kT[0]), of(t.U))])
            for h in range(2):
                units(f"RU{h}", h, [(of(t.kT[1]), of(t.B))])
            ps = begin("OUT")
            for h in range(2):
                wait_emptied(pe, t, o, f"O{h}")
            for hp in range(8):
                both = t.V[:, 2 * hp:2 * hp + 2, :].rearrange("p b n -> p (b n)")
                mm = nc.tensor.matmul(ps[:, 0:256], both, t.wo[:, hp, :], start=(hp == 0), stop=(hp == 7))
            mm.then_inc(t.sem["mm_done"], 1)

        @block.vector
        def _(dve):
            links = [0]

            def link(ins):
                links[0] += 1
                ins.then_inc(t.sem["dve_link"], 1)
                dve.wait_ge(t.sem["dve_link"], links[0])

            moe = ExpertsOnVector(nc, dve, t, o, link, finish)

            def mm(name):
                moe.through(o.place[name])
                dve.wait_ge(t.sem["front_mm" if name.rstrip("01234") in WIDE else "mm_done"], o.done[name])
                return bank(name)

            def ln_stats(i, src):
                link(nc.vector.bn_stats(t.stats[:, i, :], src))
                link(nc.vector.bn_aggr(t.mv[:, i, :], t.stats[:, i, :]))
                nc.vector.tensor_scalar(t.ln_tmp[:, i, 0:1], t.mv[:, i, 1:2], EPS, None,
                                        ALU.add).then_inc(t.sem["ln_var_ready"], 1)

            def ln_apply(i, order, dst, src):
                dve.wait_ge(t.sem["ln_guess_ready"], order)
                dve.wait_ge(t.sem["ln_var_ready"], order)
                v, r0 = t.ln_tmp[:, i, 0:1], t.ln_tmp[:, i, 2:3]
                link(nc.vector.tensor_scalar(t.ln_tmp[:, i, 3:4], v, r0, r0, ALU.mult, ALU.mult))
                link(nc.vector.tensor_scalar(t.ln_tmp[:, i, 4:5], t.ln_tmp[:, i, 3:4], -0.5, 1.5, ALU.mult, ALU.add))
                link(nc.vector.tensor_tensor(t.ln_tmp[:, i, 5:6], t.ln_tmp[:, i, 4:5], r0, ALU.mult))
                return nc.vector.tensor_scalar(dst, src, t.mv[:, i, 0:1], t.ln_tmp[:, i, 5:6],
                                               ALU.subtract, ALU.mult)

            nc.vector.tensor_copy(t.dec_end[:], t.dec[:, :, :, C - 1]).then_inc(t.sem["dec_end_ready"], 1)
            ps = mm("SB")
            nc.vector.tensor_scalar(t.sc[:, 0, :], ps[:, 0:16], K_TINY, None, ALU.max).then_inc(t.sem["norm_sq_ready"], 1)
            nc.vector.tensor_tensor(t.bgz[:], ps[:, 16:48].rearrange("p (g u) -> p g u", g=2), t.bg_bias[:],
                                    ALU.add).then_inc(t.sem["front_dve"], 1)
            ln_stats(2, t.y[:, :])
            dve.wait_ge(t.sem["norm_guess_ready"], 1)
            dve.wait_ge(t.sem["norm_sq_ready"], 1)
            link(nc.vector.tensor_tensor(t.sc[:, 3, :], t.sc[:, 0, :], t.sc[:, 2, :], ALU.mult))
            link(nc.vector.tensor_tensor(t.sc[:, 4, :], t.sc[:, 3, :], t.sc[:, 2, :], ALU.mult))
            link(nc.vector.tensor_scalar(t.sc[:, 5, :], t.sc[:, 4, :], -0.5, 1.5, ALU.mult, ALU.add))
            link(nc.vector.tensor_tensor(t.sc[:, 6, :], t.sc[:, 5, :], t.sc[:, 2, :], ALU.mult))
            dve.wait_ge(t.sem["bg_exp_ready"], 1)
            link(nc.vector.tensor_scalar(t.bg[:], t.bgz[:], 1.0, None, ALU.add))
            link(nc.vector.reciprocal(t.bg[:], t.bg[:]))
            nrm2 = over(t.sc[:, 6, :], 2)
            link(nc.vector.tensor_tensor(t.bn[:], t.bg[:], nrm2, ALU.mult))
            nc.vector.scalar_tensor_tensor(out=t.nbn2[:], in0=t.bn[:], scalar=-1.0, in1=nrm2,
                                           op0=ALU.mult, op1=ALU.mult).then_inc(t.sem["scales_ready"], 1)
            link(ln_apply(2, 1, t.y[:, :], t.y[:, :]))
            nc.vector.tensor_tensor(t.y[:], t.x_res[:], t.y[:], ALU.add).then_inc(t.sem["x2_made"], 1)
            dve.wait_ge(t.sem["x2_made"], 1)
            ln_stats(3, t.y[:, :])
            if front:
                dve.wait_ge(t.sem["x_loaded"], 32)
                ln_stats(0, t.x_new[:, :])
            if finish:
                finish_stats(nc, t, link)
                finish_apply(nc, dve, t, link)
            for s, (g, h) in enumerate(STREAMS):
                ps = mm(f"A{g}{h}")
                dve.wait_ge(t.sem["coef_ready"], s + 1)
                nc.vector.tensor_tensor(t.L[g][:, half[h], :], blk(ps[:, :]), t.L[g][:, half[h], :],
                                        ALU.mult).then_inc(t.sem["dve_emptied"], 1)
                if s == 0:
                    ln_apply(3, 2, t.xf[:, :], t.y[:, :]).then_inc(t.sem["xf_ready"], 1)
                if s == 1 and front:
                    dve.wait_ge(t.sem["res_copied"], 1)
                    link(ln_apply(0, 3, t.res_new[:, :], t.x_new[:, :]))
                    ln_stats(1, t.res_new[:, :])
            if front:
                ln_apply(1, 4, t.xhat[:, :], t.res_new[:, :]).then_inc(t.sem["xhat_ready"], 1)
            for i in range(4):
                ps = mm(f"PQ{i}")
                nc.vector.tensor_tensor(t.pqT[:, 4 * i:4 * i + 4, :, :].rearrange("p u g n -> p u (g n)"),
                                        ps[:, :].rearrange("p (u n) -> p u n", n=2 * C),
                                        over(t.pq_mask[:].rearrange("p g n -> p (g n)"), 4),
                                        ALU.mult).then_inc(t.sem["dve_emptied"], 1)
            for h in range(2):
                ps = mm(f"RQ{h}")
                nc.vector.tensor_tensor(t.rqT[:, half[h], :], blk(ps[:, :]), over(t.pq_mask[:, 1, :], 8),
                                        ALU.mult).then_inc(t.sem["dve_emptied"], 1)

            def add_gate_bias(gate, i):
                ps = mm(f"{'ar'[gate]}{i}")
                nc.vector.tensor_tensor(
                    t.z[:, gate, 512 * i:512 * i + 512].rearrange("p (m n) -> p m n", n=P),
                    ps[:, :].rearrange("p (m n) -> p m n", n=P),
                    bc(t.gate_bias[:, gate, 4 * i:4 * i + 4], P), ALU.add).then_inc(t.sem["front_dve"], 1)

            def running_sum(gate):
                dve.wait_ge(t.sem["log_ready"], gate + 1)
                nc.vector.tensor_tensor_scan(t.c[:, gate, :, :].rearrange("p u n -> p (u n)"), t.restart[:],
                                             t.z[:, gate, :], 0.0, ALU.mult, ALU.add).then_inc(t.sem["scan_done"], 1)

            for g in range(2):
                dve.wait_ge(t.sem["T0_ready"], g + 1)
                nc.vector.transpose(t.N[g][:], t.T[g][:]).then_inc(t.sem["N0_ready"], 1)
            for l in range(1, LEVELS + 1):
                for g in range(2):
                    moe.through(o.place[f"Y{l}{g}"])
                    if front and l >= 3 and g == 0:
                        running_sum(l - 3)
                    if l == 2 and g == 1:
                        wait_emptied(dve, t, o, "RL")
                        route_scores(nc, t, link)
                    if l == 3 and g == 1:
                        route_groups(nc, t, link)
                    if l == 4 and g == 1:
                        if first:
                            dve.wait_ge(t.sem["block_ready"], 1)
                        route_best(nc, t, link, slot)
                    ps = mm(f"Y{l}{g}")
                    nc.vector.tensor_tensor(t.Y[g][:], ps[:, :].rearrange("p (u n) -> p u n", n=Q),
                                            over(t.merge_mask[:, l - 1, :], 16), ALU.mult).then_inc(t.sem["dve_emptied"], 1)
                    if front and l <= 2:
                        add_gate_bias(l - 1, g)
                for g in range(2):
                    moe.through(o.place[f"N{l}{g}"])
                    wait_emptied(dve, t, o, f"N{l}{g}")
                    nc.vector.transpose(t.T[g][:], t.N[g][:]).then_inc(t.sem["T_ready"], 1)
            for h in range(2):
                ps = mm(f"KS{h}")
                link(nc.vector.tensor_tensor(t.B[:, half[h], :], blk(ps[:, :]), bc(t.nbn2[:, 0, half[h]], C),
                                             ALU.mult))
                dve.wait_ge(t.sem["bv_ready"], 1)
                nc.vector.tensor_tensor(t.B[:, half[h], :], t.B[:, half[h], :], t.bv[:, half[h], :],
                                        ALU.add).then_inc(t.sem["B_ready"], 1)
                dve.wait_ge(t.sem["B_ready"], h + 1)
                dve.sem_inc(t.sem["dve_emptied"], 1)
            for h in range(2):
                ps = mm(f"KR{h}")
                nc.vector.tensor_tensor(t.BR[:, half[h], :], blk(ps[:, :]), bc(t.nbn2[:, 1, half[h]], C),
                                        ALU.mult).then_inc(t.sem["dve_emptied"], 1)
            for h in range(2):
                ps = mm(f"PR{h}")
                nc.vector.tensor_tensor(t.bv[:, half[h], :], blk(ps[:, :]), bc(t.sc[:, 6, half[h]], C),
                                        ALU.mult).then_inc(t.sem["dve_emptied"], 1)
                if h == 1:
                    wait_emptied(dve, t, o, "PR1")
                    r, BR1 = t.bv[:, half[1], :], t.BR[:, half[1], :]
                    link(nc.vector.tensor_tensor(r, t.V[:, half[1], :], r, ALU.subtract))
                    link(nc.vector.tensor_scalar(r, r, -1.0, 1.0, ALU.max, ALU.min))
                    link(nc.vector.tensor_tensor(r, r, bc(t.bn[:, 1, half[1]], C), ALU.mult))
                    nc.vector.tensor_tensor(BR1, BR1, r, ALU.add).then_inc(t.sem["BR1_ready"], 1)
            for g, state in enumerate((t.S, t.R)):
                for h in range(2):
                    ps = mm(f"{'SR'[g]}U{h}")
                    nc.vector.tensor_tensor(state[:, half[h], :], blk(ps[:, :]), state[:, half[h], :],
                                            ALU.add).then_inc(t.sem["dve_emptied"], 1)
                    wait_emptied(dve, t, o, f"{'SR'[g]}U{h}")
                    nc.vector.tensor_tensor(state[:, half[h], :], state[:, half[h], :],
                                            bc(t.dec_end[:, g, half[h]], C), ALU.mult).then_inc(t.sem["states_ready"], 1)
            ps = mm("OUT")
            dve.wait_ge(t.sem["res_copied"], 1)
            dve.wait_ge(t.sem["x2_stored"], 16)
            nc.vector.tensor_tensor(t.y[:], ps[:, 0:256], t.res[:], ALU.add).then_inc(t.sem["dve_emptied"], 1)

        @block.scalar
        def _(act):
            links = [0]

            def link(ins):
                links[0] += 1
                ins.then_inc(t.sem["act_link"], 1)
                act.wait_ge(t.sem["act_link"], links[0])

            moe = ExpertsOnScalar(nc, act, t, o, link)

            def mm(name):
                moe.through(o.place[name])
                act.wait_ge(t.sem["front_mm" if name.rstrip("01234") in WIDE else "mm_done"], o.done[name])
                return bank(name)

            def empty(name, dst):
                ps = mm(name)
                nc.scalar.copy(dst, blk(ps[:, :])).then_inc(t.sem["act_emptied"], 1)

            def ln_guess(i, order):
                act.wait_ge(t.sem["ln_var_ready"], order)
                link(nc.scalar.activation(t.ln_tmp[:, i, 1:2], t.ln_tmp[:, i, 0:1], ACT.Ln))
                nc.scalar.activation(t.ln_tmp[:, i, 2:3], t.ln_tmp[:, i, 1:2], ACT.Exp,
                                     scale=-0.5).then_inc(t.sem["ln_guess_ready"], 1)

            act.wait_ge(t.sem["norm_sq_ready"], 1)
            link(nc.scalar.activation(t.sc[:, 1, :], t.sc[:, 0, :], ACT.Ln))
            nc.scalar.activation(t.sc[:, 2, :], t.sc[:, 1, :], ACT.Exp, scale=-0.5).then_inc(t.sem["norm_guess_ready"], 1)
            wait_emptied(act, t, o, "SB")
            nc.scalar.activation(t.bgz[:], t.bgz[:], ACT.Exp, scale=-1.0).then_inc(t.sem["bg_exp_ready"], 1)
            ln_guess(2, 1)
            for h in range(2):
                empty(f"V{h}", t.V[:, half[h], :])
            ln_guess(3, 2)
            if finish:
                finish_guess(nc, act, t, link)
            for g in range(2):
                for h in range(2):
                    empty(f"KT{g}{h}", t.kT[g][:, half[h], :])
            if front:
                ln_guess(0, 3)
            moe.through(o.place["A11"])
            if front:
                ln_guess(1, 4)
            ps = mm("RT")
            nc.scalar.copy(t.xfs[:], ps[:, 0:2 * P].rearrange("p (k n) -> p k n", n=P)).then_inc(t.sem["front_act"], 1)
            ps = mm("RL")
            nc.scalar.activation(t.score[:], ps[:, 0:E], ACT.Exp, scale=-1.0).then_inc(t.sem["front_act"], 1)
            if front:
                ps = mm("XT")
                for kt in range(2):
                    ins = nc.scalar.activation(t.xnT[:, kt, :], ps[:, P * kt:P * kt + P], ACT.Identity,
                                               bias=t.lnb[:, kt:kt + 1], scale=t.lnw[:, kt:kt + 1])
                ins.then_inc(t.sem["front_act"], 1)
            def exp_gate(gate):
                wait_emptied(act, t, o, f"{'ar'[gate]}1")
                link(nc.scalar.activation(t.z[:, gate, :], t.z[:, gate, :], ACT.Exp, scale=-1.0))
                nc.scalar.activation(t.z[:, gate, :], t.z[:, gate, :], ACT.Ln, bias=1.0).then_inc(t.sem["log_ready"], 1)

            def decays(gate):
                act.wait_ge(t.sem["scan_done"], gate + 1)
                act.wait_ge(t.sem["dec_end_ready"], 1)
                link(nc.scalar.activation(t.dec[:, gate, :, :], t.c[:, gate, :, :], ACT.Exp, scale=-1.0))
                nc.scalar.activation(t.c[:, gate, :, :], t.c[:, gate, :, :], ACT.Exp).then_inc(t.sem["dec_ready"], 1)

            def front_copy(name, dst):
                ps = mm(name)
                nc.scalar.copy(dst, blk(ps[:, :])).then_inc(t.sem["front_act"], 1)

            for l in range(1, LEVELS + 1):
                if front and l >= 3:
                    name, dst = (("k", t.k), ("q", t.q))[l - 3]
                    front_copy(f"{name}0", dst[:, half[0], :])
                    front_copy(f"{name}1", dst[:, half[1], :])
                for g in range(2):
                    ps = mm(f"N{l}{g}")
                    nc.scalar.copy(t.N[g][:], ps[:, :].rearrange("p (u n) -> p u n", n=Q)).then_inc(t.sem["act_emptied"], 1)
                if front and l in (1, 2):
                    exp_gate(l - 1)
                if front and l == 3:
                    decays(0)
            for k, dst, off in (("Z", t.Y, 0), ("X", t.inv, Q)):
                for g in range(2):
                    ps = mm(f"{k}{g}")
                    for j in range(2):
                        r = slice(C * j, C * j + Q)
                        ins = nc.scalar.copy(dst[g][r, :, off:off + Q],
                                             ps[r, :].rearrange("p (u n) -> p u n", n=Q))
                    ins.then_inc(t.sem["act_emptied"], 1)
                if front and k == "Z":
                    decays(1)
            for h in range(2):
                empty(f"U{h}", t.U[:, half[h], :])
            for h in range(2):
                empty(f"W{h}", t.B[:, half[h], :])
            for h in range(2):
                empty(f"O{h}", t.V[:, half[h], :])
            moe.through(o.last)

        @block.gpsimd
        def _(pool):
            nc.gpsimd.tensor_copy(t.res[:], t.res_new[:]).then_inc(t.sem["res_copied"], 1)
            if first:
                block_in_place(nc, pool, t)
            pool.wait_ge(t.sem["scales_ready"], 1)
            for g, h in STREAMS:
                nc.gpsimd.tensor_tensor(t.L[g][:, half[h], :], bc(t.nbn2[:, g, half[h]], C), over(t.strict[:], 8),
                                        ALU.mult).then_inc(t.sem["coef_ready"], 1)
            wait_emptied(pool, t, o, "V1")
            nc.gpsimd.tensor_tensor(t.bv[:], t.V[:], bc(t.bn[:, 0, :], C), ALU.mult).then_inc(t.sem["bv_ready"], 1)
            if finish:
                finish_add(nc, pool, t)
            for s, (g, h) in enumerate(STREAMS):
                wait_emptied(pool, t, o, f"A{g}{h}")
                nc.gpsimd.tensor_tensor(t.L[g][:, half[h], :], t.L[g][:, half[h], :], over(t.eye[:], 8),
                                        ALU.add).then_inc(t.sem["L_ready"], 1)
            pool.wait_ge(t.sem["L_ready"], 4)
            for g in range(2):
                for q in range(4):
                    r = slice(Q * q, Q * q + Q)
                    ins = nc.gpsimd.tensor_tensor(t.T[g][r, :, :], t.L[g][r, :, Q * (q % 2):Q * (q % 2) + Q],
                                                  over(t.pair_mask[r, :], 16), ALU.mult)
                ins.then_inc(t.sem["T0_ready"], 1)
            pool.wait_ge(t.sem["T0_ready"], 2)
            wait_emptied(pool, t, o, "RT")
            nc.gpsimd.tensor_copy(slot_of(t.xfT_new, 2, slot), t.xfs[:]).then_inc(t.sem["xfT_kept"], 1)
            pool.wait_ge(t.sem["xfT_kept"], 1)
            for g in range(2):
                wait_emptied(pool, t, o, f"N{LEVELS}{g}")
                for q in range(4):
                    r = slice(Q * q, Q * q + Q)
                    ins = nc.gpsimd.tensor_copy(t.inv[g][r, :, Q * (q % 2):Q * (q % 2) + Q], t.N[g][r, :, :])
                ins.then_inc(t.sem["inv_ready"], 1)
            pool.wait_ge(t.sem["inv_ready"], 2)
            def clipped_error():
                wait_emptied(pool, t, o, "PR0")
                r, BR0 = t.bv[:, half[0], :], t.BR[:, half[0], :]
                nc.gpsimd.tensor_tensor(r, t.V[:, half[0], :], r, ALU.subtract).then_inc(t.sem["pool_link"], 1)
                pool.wait_ge(t.sem["pool_link"], 1)
                nc.gpsimd.tensor_scalar(r, r, -1.0, 1.0, ALU.max, ALU.min).then_inc(t.sem["pool_link"], 1)
                pool.wait_ge(t.sem["pool_link"], 2)
                nc.gpsimd.tensor_tensor(r, r, bc(t.bn[:, 1, half[0]], C), ALU.mult).then_inc(t.sem["pool_link"], 1)
                pool.wait_ge(t.sem["pool_link"], 3)
                nc.gpsimd.tensor_tensor(BR0, BR0, r, ALU.add).then_inc(t.sem["BR0_ready"], 1)

            if not front:
                clipped_error()
            if front:
                def product(last_use, dst, a, b):
                    pool.wait_ge(t.sem["mm_done"], o.done[last_use])
                    nc.gpsimd.tensor_tensor(dst, a, b, ALU.mult).then_inc(t.sem["plus_made"], 1)

                wait_emptied(pool, t, o, "k1")
                for g in range(2):
                    pool.wait_ge(t.sem["dec_ready"], g + 1)
                    product("RQ1", t.kminus[g][:], t.k[:], t.c[:, g, :, :])
                product("KS1", t.kplus[0][:], t.k[:], t.dec[:, 0, :, :])
                product("KR1", t.kplus[1][:], t.k[:], t.dec[:, 1, :, :])
                clipped_error()
                product("PR1", t.pq[:, 0, :, 1:C], t.k[:, :, 1:C], t.dec[:, 0, :, 0:C - 1])
                nc.gpsimd.tensor_copy(t.pq[:, 0, :, 0:1], t.k[:, :, 0:1])
                product("W1", t.BR[:], t.k[:], t.k[:])
                wait_emptied(pool, t, o, "q1")
                product("O1", t.pq[:, 1, :, :], t.q[:], t.dec[:, 0, :, :])
                product("O1", t.rqplus[:], t.q[:], t.dec[:, 1, :, :])


def first_front(nc, t, X, consts, late):
    with nc.Block() as block:
        half = [slice(8 * h, 8 * h + 8) for h in range(2)]

        @block.sync
        def _(sp):
            for b in range(2):
                sp.dma_start(t.x_new[C * b:C * b + C, :], X(0, b)).then_inc(t.sem["x_loaded"], 16)
            for dst, src in consts:
                sp.dma_start(dst, src).then_inc(t.sem["consts_loaded"], 16)
            for dst, src in late:
                sp.dma_start(dst, src).then_inc(t.sem["next_loaded"], 16)
            sp.wait_ge(t.sem["consts_loaded"], 16 * len(consts))
            sp.wait_ge(t.sem["next_loaded"], 16 * len(late))

        @block.gpsimd
        def _(pool):
            nc.gpsimd.memset(t.restart[:], 1.0).then_inc(t.sem["pool_link"], 1)
            pool.wait_ge(t.sem["pool_link"], 1)
            nc.gpsimd.memset(t.restart[:].rearrange("p (u n) -> p u n", n=C)[:, :, 0:1], 0.0).then_inc(
                t.sem["restart_ready"], 1)
            nc.gpsimd.memset(t.coef[:, :, E:E + 2], 1.0)
            nc.gpsimd.memset(t.S[:], 0.0)
            nc.gpsimd.memset(t.R[:], 0.0)
            nc.gpsimd.memset(t.y[:], 0.0)
            nc.gpsimd.memset(t.x_res[:], 0.0)
            nc.gpsimd.memset(t.ones[:], 1.0)
            nc.gpsimd.memset(t.inv[0][:], 0.0)
            nc.gpsimd.memset(t.inv[1][:], 0.0)
            for g in range(2):
                pool.wait_ge(t.sem["dec_ready"], g + 1)
                nc.gpsimd.tensor_tensor(t.kminus[g][:], t.k[:], t.c[:, g, :, :], ALU.mult)
                nc.gpsimd.tensor_tensor(t.kplus[g][:], t.k[:], t.dec[:, g, :, :], ALU.mult)
            nc.gpsimd.tensor_copy(t.pq[:, 0, :, 0:1], t.k[:, :, 0:1])
            nc.gpsimd.tensor_tensor(t.pq[:, 0, :, 1:C], t.k[:, :, 1:C], t.dec[:, 0, :, 0:C - 1], ALU.mult)
            nc.gpsimd.tensor_tensor(t.BR[:], t.k[:], t.k[:], ALU.mult)
            nc.gpsimd.tensor_tensor(t.pq[:, 1, :, :], t.q[:], t.dec[:, 0, :, :], ALU.mult)
            nc.gpsimd.tensor_tensor(t.rqplus[:], t.q[:], t.dec[:, 1, :, :], ALU.mult)

        @block.vector
        def _(dve):
            links = [0]

            def link(ins):
                links[0] += 1
                ins.then_inc(t.sem["dve_link"], 1)
                dve.wait_ge(t.sem["dve_link"], links[0])

            dve.wait_ge(t.sem["x_loaded"], 32)
            for i, (src, dst) in enumerate(((t.x_new, t.res_new), (t.res_new, t.xhat))):
                link(nc.vector.bn_stats(t.stats[:, i, :], src[:, :]))
                link(nc.vector.bn_aggr(t.mv[:, i, :], t.stats[:, i, :]))
                nc.vector.tensor_scalar(t.ln_tmp[:, i, 0:1], t.mv[:, i, 1:2], EPS, None,
                                        ALU.add).then_inc(t.sem["ln_var_ready"], 1)
                dve.wait_ge(t.sem["ln_guess_ready"], i + 1)
                dve.wait_ge(t.sem["ln_var_ready"], i + 1)
                v, r0 = t.ln_tmp[:, i, 0:1], t.ln_tmp[:, i, 2:3]
                link(nc.vector.tensor_scalar(t.ln_tmp[:, i, 3:4], v, r0, r0, ALU.mult, ALU.mult))
                link(nc.vector.tensor_scalar(t.ln_tmp[:, i, 4:5], t.ln_tmp[:, i, 3:4], -0.5, 1.5, ALU.mult, ALU.add))
                link(nc.vector.tensor_tensor(t.ln_tmp[:, i, 5:6], t.ln_tmp[:, i, 4:5], r0, ALU.mult))
                ins = nc.vector.tensor_scalar(dst[:, :], src[:, :], t.mv[:, i, 0:1], t.ln_tmp[:, i, 5:6],
                                              ALU.subtract, ALU.mult)
                if i == 0:
                    link(ins)
                else:
                    ins.then_inc(t.sem["xhat_ready"], 1)
            dve.wait_ge(t.sem["consts_loaded"], 16 * len(consts))
            for gate in range(2):
                for i in range(2):
                    name = f"{'ar'[gate]}{i}"
                    dve.wait_ge(t.sem["front_mm"], 1 + 2 * gate + i + 1)
                    nc.vector.tensor_tensor(
                        t.z[:, gate, 512 * i:512 * i + 512].rearrange("p (m n) -> p m n", n=P),
                        t.ps[2 * gate + i][:, :].rearrange("p (m n) -> p m n", n=P),
                        bc(t.gate_bias[:, gate, 4 * i:4 * i + 4], P), ALU.add).then_inc(t.sem["front_dve"], 1)
            dve.wait_ge(t.sem["restart_ready"], 1)
            for gate in range(2):
                dve.wait_ge(t.sem["log_ready"], gate + 1)
                nc.vector.tensor_tensor_scan(t.c[:, gate, :, :].rearrange("p u n -> p (u n)"), t.restart[:],
                                             t.z[:, gate, :], 0.0, ALU.mult, ALU.add).then_inc(t.sem["scan_done"], 1)

        @block.tensor
        def _(pe):
            pe.wait_ge(t.sem["consts_loaded"], 16 * len(consts))
            pe.wait_ge(t.sem["xhat_ready"], 1)
            for kt in range(2):
                mm = nc.tensor.transpose(t.ps[6][:, P * kt:P * kt + P], t.xhat[:, P * kt:P * kt + P], t.ident[:, :])
            mm.then_inc(t.sem["front_mm"], 1)
            pe.wait_ge(t.sem["front_act"], 1)
            for f, w in enumerate((t.wa, t.war, t.wk)):
                for i in range(2):
                    for m in range(4):
                        for kt in range(2):
                            hp = 4 * i + m
                            mm = nc.tensor.matmul(t.ps[2 * f + i][:, P * m:P * m + P], w[:, kt, P * hp:P * hp + P],
                                                  t.xnT[:, kt, :], start=(kt == 0), stop=(kt == 1))
                    mm.then_inc(t.sem["front_mm"], 1)
            for i in range(2):
                for m in range(4):
                    for kt in range(2):
                        hp = 4 * i + m
                        mm = nc.tensor.matmul(t.ps[6 + i][:, P * m:P * m + P], t.wq[:, kt, P * hp:P * hp + P],
                                              t.xnT[:, kt, :], start=(kt == 0), stop=(kt == 1))
                mm.then_inc(t.sem["front_mm"], 1)

        @block.scalar
        def _(act):
            links = [0]

            def link(ins):
                links[0] += 1
                ins.then_inc(t.sem["act_link"], 1)
                act.wait_ge(t.sem["act_link"], links[0])

            nc.scalar.preload_act_table_set("natural_log_exp_and_others")
            for i in range(2):
                act.wait_ge(t.sem["ln_var_ready"], i + 1)
                link(nc.scalar.activation(t.ln_tmp[:, i, 1:2], t.ln_tmp[:, i, 0:1], ACT.Ln))
                nc.scalar.activation(t.ln_tmp[:, i, 2:3], t.ln_tmp[:, i, 1:2], ACT.Exp,
                                     scale=-0.5).then_inc(t.sem["ln_guess_ready"], 1)
            act.wait_ge(t.sem["consts_loaded"], 16 * len(consts))
            act.wait_ge(t.sem["front_mm"], 1)
            for kt in range(2):
                ins = nc.scalar.activation(t.xnT[:, kt, :], t.ps[6][:, P * kt:P * kt + P], ACT.Identity,
                                           bias=t.lnb[:, kt:kt + 1], scale=t.lnw[:, kt:kt + 1])
            ins.then_inc(t.sem["front_act"], 1)
            for gate in range(2):
                act.wait_ge(t.sem["front_dve"], 2 * gate + 2)
                link(nc.scalar.activation(t.z[:, gate, :], t.z[:, gate, :], ACT.Exp, scale=-1.0))
                nc.scalar.activation(t.z[:, gate, :], t.z[:, gate, :], ACT.Ln, bias=1.0).then_inc(t.sem["log_ready"], 1)
            for h in range(2):
                act.wait_ge(t.sem["front_mm"], 5 + h + 1)
                nc.scalar.copy(t.k[:, half[h], :], blk(t.ps[4 + h][:, :]))
            for h in range(2):
                act.wait_ge(t.sem["front_mm"], 7 + h + 1)
                ins = nc.scalar.copy(t.q[:, half[h], :], blk(t.ps[6 + h][:, :]))
            for gate in range(2):
                act.wait_ge(t.sem["scan_done"], gate + 1)
                link(nc.scalar.activation(t.dec[:, gate, :, :], t.c[:, gate, :, :], ACT.Exp, scale=-1.0))
                nc.scalar.activation(t.c[:, gate, :, :], t.c[:, gate, :, :], ACT.Exp).then_inc(t.sem["dec_ready"], 1)


def last_tile(nc, t, slot, scratch_slot):
    with nc.Block() as block:
        @block.vector
        def _(dve):
            links = [0]

            def link(ins):
                links[0] += 1
                ins.then_inc(t.sem["dve_link"], 1)
                dve.wait_ge(t.sem["dve_link"], links[0])

            def layernorm(i, order, dst, src):
                link(nc.vector.bn_stats(t.stats[:, i, :], src))
                link(nc.vector.bn_aggr(t.mv[:, i, :], t.stats[:, i, :]))
                nc.vector.tensor_scalar(t.ln_tmp[:, i, 0:1], t.mv[:, i, 1:2], EPS, None,
                                        ALU.add).then_inc(t.sem["ln_var_ready"], 1)
                dve.wait_ge(t.sem["ln_guess_ready"], order)
                dve.wait_ge(t.sem["ln_var_ready"], order)
                v, r0 = t.ln_tmp[:, i, 0:1], t.ln_tmp[:, i, 2:3]
                link(nc.vector.tensor_scalar(t.ln_tmp[:, i, 3:4], v, r0, r0, ALU.mult, ALU.mult))
                link(nc.vector.tensor_scalar(t.ln_tmp[:, i, 4:5], t.ln_tmp[:, i, 3:4], -0.5, 1.5, ALU.mult, ALU.add))
                link(nc.vector.tensor_tensor(t.ln_tmp[:, i, 5:6], t.ln_tmp[:, i, 4:5], r0, ALU.mult))
                return nc.vector.tensor_scalar(dst, src, t.mv[:, i, 0:1], t.ln_tmp[:, i, 5:6], ALU.subtract, ALU.mult)

            link(layernorm(2, 1, t.y[:, :], t.y[:, :]))
            nc.vector.tensor_tensor(t.y[:], t.x_res[:], t.y[:], ALU.add).then_inc(t.sem["x2_made"], 1)
            dve.wait_ge(t.sem["x2_made"], 1)
            layernorm(3, 2, t.xf[:, :], t.y[:, :]).then_inc(t.sem["xf_ready"], 1)
            dve.wait_ge(t.sem["front_act"], 2)
            route_scores(nc, t, link)
            route_groups(nc, t, link)
            route_best(nc, t, link, slot)

        @block.scalar
        def _(act):
            for i in (2, 3):
                act.wait_ge(t.sem["ln_var_ready"], i - 1)
                nc.scalar.activation(t.ln_tmp[:, i, 1:2], t.ln_tmp[:, i, 0:1], ACT.Ln).then_inc(t.sem["act_link"], 1)
                act.wait_ge(t.sem["act_link"], i - 1)
                nc.scalar.activation(t.ln_tmp[:, i, 2:3], t.ln_tmp[:, i, 1:2], ACT.Exp,
                                     scale=-0.5).then_inc(t.sem["ln_guess_ready"], 1)
            act.wait_ge(t.sem["front_mm"], 1)
            nc.scalar.copy(t.xfs[:], t.ps[0][:, 0:2 * P].rearrange("p (k n) -> p k n", n=P)).then_inc(
                t.sem["front_act"], 1)
            act.wait_ge(t.sem["front_mm"], 2)
            nc.scalar.activation(t.score[:], t.ps[1][:, 0:E], ACT.Exp, scale=-1.0).then_inc(t.sem["front_act"], 1)

        @block.tensor
        def _(pe):
            pe.wait_ge(t.sem["xf_ready"], 1)
            for kt in range(2):
                mm = nc.tensor.transpose(t.ps[0][:, P * kt:P * kt + P], t.xf[:, P * kt:P * kt + P], t.ident[:, :])
            mm.then_inc(t.sem["front_mm"], 1)
            pe.wait_ge(t.sem["front_act"], 1)
            for kt in range(2):
                mm = nc.tensor.matmul(t.ps[1][:, 0:E], t.xfs[:, kt, :], t.rw[:, kt, :], start=(kt == 0), stop=(kt == 1))
            mm.then_inc(t.sem["front_mm"], 1)

        @block.sync
        def _(sp):
            sp.wait_ge(t.sem["x2_made"], 1)
            sp.dma_start(scratch_slot, t.y[:, :]).then_inc(t.sem["x2_stored"], 16)
            sp.wait_ge(t.sem["x2_stored"], 16)

        @block.gpsimd
        def _(pool):
            pool.wait_ge(t.sem["front_act"], 1)
            nc.gpsimd.tensor_copy(slot_of(t.xfT_new, 2, slot), t.xfs[:]).then_inc(t.sem["xfT_kept"], 1)


def experts_alone(nc, t, a, first, count):
    SLOTS = 8
    wg, wu = ([w[:, :, P * i:P * i + P] for i in range(SLOTS)] for w in (t.wa, t.war))
    wd = [t.wk[:].rearrange("p k n -> p (k n)")[:, 256 * i:256 * i + 256] for i in range(SLOTS)]
    g_bank, u_bank, y_bank = (4, 0), (5, 1), (6, 2)
    h = (t.h[:], t.L[0][:, 0:8, :].rearrange("p u n -> p (u n)"))
    with nc.Block() as block:
        @block.sync
        def _(sp):
            for i in range(count):
                if i >= SLOTS:
                    sp.wait_ge(t.sem["y_done"], 2 * (i - SLOTS + 1))
                if i >= 1:
                    sp.wait_ge(t.sem["weights_loaded"], 48 * i)
                load_expert(sp, a, wg[i % SLOTS], wu[i % SLOTS], wd[i % SLOTS], first + i, t.sem["weights_loaded"])
            sp.wait_ge(t.sem["weights_loaded"], 48 * count)

        @block.gpsimd
        def _(pool):
            src = t.coef[:, :, first:first + count] if isinstance(first, int) else t.coef[:, :, bass.ds(first, count)]
            nc.gpsimd.tensor_copy(t.coef_run[:, :, 0:count], src).then_inc(t.sem["coef_ready"], 1)

        @block.tensor
        def _(pe):
            for i in range(count + 1):
                if i < count:
                    pe.wait_ge(t.sem["weights_loaded"], 48 * (i + 1))
                    if i >= 2:
                        pe.wait_ge(t.sem["h_ready"], i - 1)
                    for w, bank, done in ((wg, g_bank, "g_done"), (wu, u_bank, "u_done")):
                        for kt in range(2):
                            mm = nc.tensor.matmul(t.ps[bank[i % 2]][:, :], w[i % SLOTS][:, kt, :],
                                                  t.xfT[:, kt, :, :].rearrange("p m n -> p (m n)"),
                                                  start=(kt == 0), stop=(kt == 1))
                        mm.then_inc(t.sem[done], 1)
                if i >= 1:
                    k = i - 1
                    pe.wait_ge(t.sem["h_ready"], k + 1)
                    for m in range(4):
                        if m % 2 == 0 and k >= 2:
                            pe.wait_ge(t.sem["y_added"], 2 * (k - 2) + m // 2 + 1)
                        mm = nc.tensor.matmul(t.ps[y_bank[k % 2] + m // 2][:, 256 * (m % 2):256 * (m % 2) + 256],
                                              h[k % 2][:, P * m:P * m + P], wd[k % SLOTS], start=True, stop=True)
                        if m % 2 == 1:
                            mm.then_inc(t.sem["y_done"], 1)

        @block.scalar
        def _(act):
            links = [0]

            def link(ins):
                links[0] += 1
                ins.then_inc(t.sem["act_link"], 1)
                act.wait_ge(t.sem["act_link"], links[0])

            for i in range(count):
                act.wait_ge(t.sem["g_done"], i + 1)
                if i >= 2:
                    act.wait_ge(t.sem["y_done"], 2 * (i - 1))
                link(nc.scalar.activation(h[i % 2], t.ps[g_bank[i % 2]][:, :], ACT.Exp, scale=-1.0))
                link(nc.scalar.activation(h[i % 2], h[i % 2], ACT.Ln, bias=1.0))
                nc.scalar.activation(h[i % 2], h[i % 2], ACT.Exp, scale=-1.0).then_inc(t.sem["sig_ready"], 1)

        @block.vector
        def _(dve):
            dve.wait_ge(t.sem["coef_ready"], 1)
            for i in range(count + 1):
                if i < count:
                    dve.wait_ge(t.sem["sig_ready"], i + 1)
                    nc.vector.tensor_tensor(h[i % 2], t.ps[g_bank[i % 2]][:, :], h[i % 2],
                                            ALU.mult).then_inc(t.sem["dve_link"], 1)
                    dve.wait_ge(t.sem["dve_link"], i + 1)
                    dve.wait_ge(t.sem["u_done"], i + 1)
                    nc.vector.tensor_tensor(h[i % 2], t.ps[u_bank[i % 2]][:, :], h[i % 2],
                                            ALU.mult).then_inc(t.sem["h_ready"], 1)
                if i >= 1:
                    k = i - 1
                    for m in range(4):
                        if m % 2 == 0:
                            dve.wait_ge(t.sem["y_done"], 2 * k + m // 2 + 1)
                            if k >= 1:
                                dve.wait_ge(t.sem["y_added"], 2 * (k - 1) + m // 2 + 1)
                        ins = nc.vector.scalar_tensor_tensor(
                            out=t.acc[:, m, :], in0=t.ps[y_bank[k % 2] + m // 2][:, 256 * (m % 2):256 * (m % 2) + 256],
                            scalar=t.coef_run[:, m, k:k + 1], in1=t.acc[:, m, :], op0=ALU.mult, op1=ALU.add)
                        if m % 2 == 1:
                            ins.then_inc(t.sem["y_added"], 1)


def start_last_block(nc, t):
    with nc.Block() as block:
        @block.gpsimd
        def _(pool):
            block_in_place(nc, pool, t)

        @block.vector
        def _(dve):
            nc.vector.memset(t.acc[:], 0.0).then_inc(t.sem["dve_link"], 1)
            dve.wait_ge(t.sem["dve_link"], 1)


def finish_stats(nc, t, link):
    for m in range(4):
        ins = nc.vector.bn_stats(t.fin_stats[:, m, :], t.acc[:, m, :])
    link(ins)
    for m in range(4):
        ins = nc.vector.bn_aggr(t.fin_mv[:, m, :], t.fin_stats[:, m, :])
    link(ins)
    nc.vector.tensor_scalar(t.fin_tmp[:, 0, :], t.fin_mv[:, :, 1], EPS, None, ALU.add).then_inc(t.sem["fin_var"], 1)


def finish_guess(nc, act, t, link):
    act.wait_ge(t.sem["fin_var"], 1)
    link(nc.scalar.activation(t.fin_tmp[:, 1, :], t.fin_tmp[:, 0, :], ACT.Ln))
    nc.scalar.activation(t.fin_tmp[:, 2, :], t.fin_tmp[:, 1, :], ACT.Exp, scale=-0.5).then_inc(t.sem["fin_guess"], 1)


def finish_apply(nc, dve, t, link):
    var, r0, step, rstd = (t.fin_tmp[:, i, :] for i in (0, 2, 3, 4))
    dve.wait_ge(t.sem["fin_guess"], 1)
    dve.wait_ge(t.sem["fin_var"], 1)
    link(nc.vector.tensor_tensor(step, var, r0, ALU.mult))
    link(nc.vector.tensor_tensor(step, step, r0, ALU.mult))
    link(nc.vector.tensor_scalar(step, step, -0.5, 1.5, ALU.mult, ALU.add))
    link(nc.vector.tensor_tensor(rstd, step, r0, ALU.mult))
    for m in range(4):
        nc.vector.tensor_scalar(t.acc[:, m, :], t.acc[:, m, :], t.fin_mv[:, m, 0:1], rstd[:, m:m + 1],
                                ALU.subtract, ALU.mult).then_inc(t.sem["fin_rows"], 1)


def finish_add(nc, pool, t):
    pool.wait_ge(t.sem["x2_loaded"], 16)
    for m in range(4):
        pool.wait_ge(t.sem["fin_rows"], m + 1)
        nc.gpsimd.tensor_tensor(t.rows[:, m, :], t.acc[:, m, :], t.rows[:, m, :], ALU.add).then_inc(
            t.sem["fin_added"], 1)


def finish_load(sp, t, x2_rows, b):
    src = x2_rows[4 * b + 1:4 * b + 5] if isinstance(b, int) else x2_rows[bass.ds(b * 4 + 1, 4)]
    sp.dma_start(t.rows[:], src.rearrange("n p d -> p n d")).then_inc(t.sem["x2_loaded"], 16)


def finish_store(sp, t, out, b):
    Ov = out.rearrange("b (n t) d -> b t n d", t=C)
    sp.wait_ge(t.sem["fin_added"], 4)
    for s in range(2):
        dst = Ov[s][:, 4 * b:4 * b + 4, :] if isinstance(b, int) else Ov[s][:, bass.ds(b * 4, 4), :]
        sp.dma_start(dst, t.rows[C * s:C * s + C, :, :]).then_inc(t.sem["out_stored"], 16)


def finish_block(nc, t, out, x2_rows, b):
    with nc.Block() as block:
        @block.vector
        def _(dve):
            links = [0]

            def link(ins):
                links[0] += 1
                ins.then_inc(t.sem["dve_link"], 1)
                dve.wait_ge(t.sem["dve_link"], links[0])

            finish_stats(nc, t, link)
            finish_apply(nc, dve, t, link)

        @block.scalar
        def _(act):
            def link(ins):
                ins.then_inc(t.sem["act_link"], 1)
                act.wait_ge(t.sem["act_link"], 1)

            finish_guess(nc, act, t, link)

        @block.gpsimd
        def _(pool):
            finish_add(nc, pool, t)

        @block.sync
        def _(sp):
            finish_load(sp, t, x2_rows, b)
            finish_store(sp, t, out, b)
            sp.wait_ge(t.sem["out_stored"], 32)


def clear(nc, sems):
    nc.gpsimd.sem_clear(range(sems[0].num, sems[-1].num + 1))
    nc.all_engine_barrier()


def program(nc, a, out):
    chunks = a["x"].shape[1] // C
    blocks = chunks // 4
    Xv = a["x"].rearrange("b (n t) d -> n b t d", t=C)
    x2_rows = nc.dram_tensor("x2_rows", (chunks + 1, P, 256), F32, kind="Internal").ap()
    with ExitStack() as ctx:
        t = alloc_attention(nc, ctx)

        def scratch(n):
            if isinstance(n, int):
                return x2_rows[n]
            return x2_rows[bass.ds(n, 1)].rearrange("o p d -> (o p) d")

        def X(n, b):
            if isinstance(n, int):
                return Xv[n, b]
            return Xv[bass.ds(n, 1), b].rearrange("o t d -> (o t) d")

        def group_body(n, m, front=True, prefetch=True, finish=None):
            body(nc, t, a, n, X, scratch, m + 1, front, GROUPS[m], first=(m == 0),
                 prefetch=GROUPS[(m + 1) % 4][0] if prefetch else None, finish=finish)
            clear(nc, t.sems)

        consts = [(t.lnw[:], a["lnw"]), (t.lnb[:], a["lnb"]), (t.ident[:], a["ident"]), (t.wa[:], a["wa"]),
                  (t.gate_bias[:], a["gate_bias"]), (t.war[:], a["war"]), (t.wk[:], a["wk"]), (t.wq[:], a["wq"]),
                  (t.bg_bias[:], a["bg_bias"])]
        late = [(t.wv[:], a["wv"]), (t.wo[:], a["wo"]), (t.wbg[:], a["wbg"]),
                (t.eye[:], a["eye"]), (t.strict[:], a["strict"]), (t.pair_mask[:], a["pair_mask"]),
                (t.merge_mask[:], a["merge_mask"]), (t.pq_mask[:], a["pq_mask"]),
                (t.rw[:], a["rw"]), (t.e_bias[:], a["e_bias"]),
                (t.wg[:, 0, :, :], a["wg"][0].rearrange("(k p) i -> p k i", p=P)),
                (t.wu[:, 0, :, :], a["wu"][0].rearrange("(k p) i -> p k i", p=P)), (t.wd[:, 0, :], a["wd"][0])]
        first_front(nc, t, X, consts, late)
        clear(nc, t.sems)
        with nc.Fori(0, 5) as n:
            body(nc, t, a, n, X, scratch, n, True)
            clear(nc, t.sems)
        group_body(5, 0)
        with nc.Fori(0, blocks - 2) as b:
            for m in range(1, 4):
                group_body(b * 4 + (5 + m), m)
            group_body(b * 4 + 9, 0, finish=(out, x2_rows, b))
        group_body(chunks - 2, 1)
        group_body(chunks - 1, 2, front=False, prefetch=False)
        last_tile(nc, t, 4, scratch(chunks))
        clear(nc, t.sems)
        experts_alone(nc, t, a, GROUPS[3][0], len(GROUPS[3]))
        clear(nc, t.sems)
        finish_block(nc, t, out, x2_rows, blocks - 2)
        clear(nc, t.sems)
        start_last_block(nc, t)
        clear(nc, t.sems)
        with nc.Fori(0, (E + 2) // RUN) as i:
            experts_alone(nc, t, a, i * RUN, RUN)
            clear(nc, t.sems)
        finish_block(nc, t, out, x2_rows, blocks - 1)
        clear(nc, t.sems)


def layouts(np, d):
    def f(name):
        return np.asarray(d[name])

    def kt(w):
        return w.T.reshape(2, P, -1).transpose(1, 0, 2)

    a = {}
    a["x"] = f("L0_attn_x")
    a["wq"], a["wk"], a["wa"], a["war"] = (kt(f("L0_attn_" + n)) for n in ("Wq", "Wk", "Wa", "WaR"))
    wv = kt(f("L0_attn_Wv")).reshape(P, 2, 8, 2, C)
    a["wv"] = wv.transpose(0, 1, 3, 2, 4).reshape(P, 2, 2, 512)
    a["wo"] = f("L0_attn_Wo").T.reshape(8, P, 256).transpose(1, 0, 2)
    bg = np.stack([f("L0_attn_Wb"), f("L0_attn_Wg")])
    bg = bg.reshape(2, 8, 2, 2, P)
    a["wbg"] = bg.transpose(4, 3, 2, 0, 1).reshape(P, 2, 2, 16)
    gb = np.stack([f("L0_attn_ba"), f("L0_attn_baR")]).reshape(2, 8, P)
    a["gate_bias"] = gb.transpose(2, 0, 1)
    b2 = np.stack([f("L0_attn_bb"), f("L0_attn_bg")]).reshape(2, 8, 2).transpose(2, 0, 1)
    a["bg_bias"] = np.broadcast_to(b2[:, None, :, :, None], (2, C, 2, 8, 2)).reshape(P, 2, 16)
    a["lnw"], a["lnb"] = f("L0_attn_ln_w").reshape(2, P).T, f("L0_attn_ln_b").reshape(2, P).T
    a["rw"] = f("L0_ffn_router_w").T.reshape(2, P, E).transpose(1, 0, 2)
    a["e_bias"] = np.broadcast_to(f("L0_ffn_e_bias")[None, :], (P, E))
    for n, s in (("wg", "SWg"), ("wu", "SWu")):
        shared = f("L0_ffn_" + s).reshape(256, 2, P).transpose(1, 0, 2)
        a[n] = np.concatenate([f("L0_ffn_W" + n[1]), shared])
    a["wd"] = np.concatenate([f("L0_ffn_Wd"), f("L0_ffn_SWd").reshape(2, P, 256)])

    r, c = np.arange(C)[:, None], np.arange(C)[None, :]
    two = lambda m: np.concatenate([m, m]).astype(np.float32)
    a["ident"] = np.eye(P, dtype=np.float32)
    a["eye"] = two(r == c)
    a["strict"] = two(r > c)
    a["pair_mask"] = two((r // 2 == c // 2) & (r >= c))[:, 0:Q] + two((r // 2 == c // 2) & (r >= c))[:, Q:C]
    m = [(r == c) | ((r // (2 * b) == c // (2 * b)) & (r // b % 2 == 0) & (c // b % 2 == 1)) for b in (2, 4, 8, 16)]
    a["merge_mask"] = np.stack([two(x)[:, 0:Q] + two(x)[:, Q:C] for x in m], axis=1)
    a["pq_mask"] = np.stack([two(r < c), two(r <= c)], axis=1)
    return {k: np.ascontiguousarray(v) for k, v in a.items()}


def kernel(**inputs):
    import numpy as _np
    import concourse.bacc as _bacc
    from concourse import mybir as _mybir
    from concourse.bass_utils import run_bass_kernel_spmd as _run

    nc = _bacc.Bacc("TRN2", target_bir_lowering=False, num_devices=1)
    arrays, aps = {}, {}
    for name, arr in layouts(_np, inputs).items():
        arrays[f"in_{name}_dram"] = arr
        aps[name] = nc.dram_tensor(f"in_{name}_dram", arr.shape, _mybir.dt.from_np(arr.dtype), kind="ExternalInput").ap()
    out = nc.dram_tensor("out_0_dram", (2, 2048, 256), _mybir.dt.float32, kind="ExternalOutput").ap()
    program(nc, aps, out)
    r = _run(nc, [arrays], core_ids=[0])
    return r.results[0]["out_0_dram"]
```
